# Optimizing a Trainium2 kernel written in Bass

```python
import numpy as np
import jax
import jax.numpy as jnp

def _softmax(x, axis=-1):
    return jax.nn.softmax(x, axis=axis)

def _gelu(x):
    return jax.nn.gelu(x, approximate=True)

def _silu(x):
    return jax.nn.silu(x)

def _sigmoid(x):
    return jax.nn.sigmoid(x)

def _layernorm(x, axis=-1, eps=1e-05):
    m = jnp.mean(x, axis=axis, keepdims=True)
    v = jnp.var(x, axis=axis, keepdims=True)
    return (x - m) / jnp.sqrt(v + eps)

def _scatter_add(tgt, idx, src, axis=0):
    return tgt.at[idx].add(src)

def _segment_sum(src, seg, n):
    return jax.ops.segment_sum(src, seg, n)
kernel_name = 'mk_seq_postln_d1_jaxref_r8_fe37eb'

def setup_inputs(seed: int=0):
    np.random.seed(seed)
    _w = jnp.asarray

    def _L0_attn_setup():
        import jax, jax.numpy as jnp
        import numpy as np
        DM = 128
        DI = 256
        DS = 16
        DC = 4
        DR = 64
        BATCH = 2
        SEQ = 128
        EPS = 1e-05
        key = jax.random.key(seed)
        ks = jax.random.split(key, 8)
        s = 0.02
        dt = jnp.exp(jax.random.uniform(ks[5], (DI,)) * (np.log(0.1) - np.log(0.001)) + np.log(0.001))
        dt_bias = jnp.log(jnp.expm1(dt))
        return {'hidden_states': jax.random.normal(ks[0], (BATCH, SEQ, DM), jnp.float32), 'norm_w': jnp.ones((DM,), jnp.float32), 'norm_b': jnp.zeros((DM,), jnp.float32), 'in_proj_w': jax.random.normal(ks[1], (2 * DI, DM), jnp.float32) * s, 'conv_w': jax.random.normal(ks[2], (DI, 1, DC), jnp.float32) * s, 'conv_b': jnp.zeros((DI,), jnp.float32), 'x_proj_w': jax.random.normal(ks[3], (DR + 2 * DS, DI), jnp.float32) * s, 'dt_proj_w': jax.random.normal(ks[4], (DI, DR), jnp.float32) * DR ** (-0.5), 'dt_proj_b': dt_bias, 'A_log': jnp.log(jnp.tile(jnp.arange(1, DS + 1, dtype=jnp.float32), (DI, 1))), 'D': jnp.ones((DI,), jnp.float32), 'out_proj_w': jax.random.normal(ks[6], (DM, DI), jnp.float32) * s}
    _L0_attn_in = _L0_attn_setup()

    def _L0_ffn_setup():
        import jax, jax.numpy as jnp
        import numpy as np
        B, S, D = (4, 256, 128)
        P = 9
        DM = D // 4
        EPS = 1e-05

        def _mix(x, mix_kernel):
            xp = jnp.pad(x, ((0, 0), (1, 1), (0, 0)))
            return mix_kernel[0] * xp[:, :-2] + mix_kernel[1] * xp[:, 1:-1] + mix_kernel[2] * xp[:, 2:]

        def _layernorm(h, gamma, beta):
            mu = jnp.mean(h, axis=-1, keepdims=True)
            var = jnp.var(h, axis=-1, keepdims=True)
            return (h - mu) * jax.lax.rsqrt(var + EPS) * gamma + beta
        key = jax.random.key(seed)
        ks = jax.random.split(key, 12)
        sc_in = 1.0 / np.sqrt(D)
        sc_mid = 1.0 / np.sqrt(DM)
        return {'x': jax.random.normal(ks[0], (B, S, D), dtype=jnp.float32), 'mix_kernel': jax.random.normal(ks[1], (3, D), dtype=jnp.float32) * 0.5, 'W1': jax.random.normal(ks[2], (P, D, DM), dtype=jnp.float32) * sc_in, 'b1': jnp.zeros((P, DM), dtype=jnp.float32), 'W2': jax.random.normal(ks[3], (P, DM, D), dtype=jnp.float32) * sc_mid, 'b2': jnp.zeros((P, D), dtype=jnp.float32), 'Wo1': jax.random.normal(ks[4], (D, DM), dtype=jnp.float32) * sc_in, 'bo1': jnp.zeros((DM,), dtype=jnp.float32), 'Wo2': jax.random.normal(ks[5], (DM, P), dtype=jnp.float32) * sc_mid, 'bo2': jnp.zeros((P,), dtype=jnp.float32), 'gamma': jnp.ones((D,), dtype=jnp.float32), 'beta': jnp.zeros((D,), dtype=jnp.float32)}
    _L0_ffn_in = _L0_ffn_setup()
    _d = {'L0_attn_hidden_states': _L0_attn_in['hidden_states'], 'L0_attn_norm_w': _L0_attn_in['norm_w'], 'L0_attn_norm_b': _L0_attn_in['norm_b'], 'L0_attn_in_proj_w': _L0_attn_in['in_proj_w'], 'L0_attn_conv_w': _L0_attn_in['conv_w'], 'L0_attn_conv_b': _L0_attn_in['conv_b'], 'L0_attn_x_proj_w': _L0_attn_in['x_proj_w'], 'L0_attn_dt_proj_w': _L0_attn_in['dt_proj_w'], 'L0_attn_dt_proj_b': _L0_attn_in['dt_proj_b'], 'L0_attn_A_log': _L0_attn_in['A_log'], 'L0_attn_D': _L0_attn_in['D'], 'L0_attn_out_proj_w': _L0_attn_in['out_proj_w'], 'L0_ffn_mix_kernel': _L0_ffn_in['mix_kernel'], 'L0_ffn_W1': _L0_ffn_in['W1'], 'L0_ffn_b1': _L0_ffn_in['b1'], 'L0_ffn_W2': _L0_ffn_in['W2'], 'L0_ffn_b2': _L0_ffn_in['b2'], 'L0_ffn_Wo1': _L0_ffn_in['Wo1'], 'L0_ffn_bo1': _L0_ffn_in['bo1'], 'L0_ffn_Wo2': _L0_ffn_in['Wo2'], 'L0_ffn_bo2': _L0_ffn_in['bo2'], 'L0_ffn_gamma': _L0_ffn_in['gamma'], 'L0_ffn_beta': _L0_ffn_in['beta']}
    _x0 = _d['L0_attn_hidden_states']
    _d['L0_attn_hidden_states'] = jax.random.normal(jax.random.fold_in(jax.random.key(seed), 1), (8, 1024, 128), dtype=_x0.dtype)
    del _x0
    return _d

def reference(L0_attn_hidden_states, L0_attn_norm_w, L0_attn_norm_b, L0_attn_in_proj_w, L0_attn_conv_w, L0_attn_conv_b, L0_attn_x_proj_w, L0_attn_dt_proj_w, L0_attn_dt_proj_b, L0_attn_A_log, L0_attn_D, L0_attn_out_proj_w, L0_ffn_mix_kernel, L0_ffn_W1, L0_ffn_b1, L0_ffn_W2, L0_ffn_b2, L0_ffn_Wo1, L0_ffn_bo1, L0_ffn_Wo2, L0_ffn_bo2, L0_ffn_gamma, L0_ffn_beta):

    def _L0_attn_ref(hidden_states, norm_w, norm_b, in_proj_w, conv_w, conv_b, x_proj_w, dt_proj_w, dt_proj_b, A_log, D, out_proj_w):
        import jax, jax.numpy as jnp
        import numpy as np
        DM = 128
        DI = 256
        DS = 16
        DC = 4
        DR = 64
        BATCH = 2
        SEQ = 128
        EPS = 1e-05
        residual = hidden_states
        mu = jnp.mean(hidden_states, -1, keepdims=True)
        var = jnp.mean(jnp.square(hidden_states - mu), -1, keepdims=True)
        h = (hidden_states - mu) * jax.lax.rsqrt(var + EPS) * norm_w + norm_b
        xz = h @ in_proj_w.T
        x, z = jnp.split(xz, 2, axis=-1)
        xc = jnp.transpose(x, (0, 2, 1))
        xc = jax.lax.conv_general_dilated(xc, conv_w, (1,), [(DC - 1, 0)], dimension_numbers=('NCH', 'OIH', 'NCH'), feature_group_count=DI)
        xc = xc + conv_b[None, :, None]
        x = jax.nn.silu(jnp.transpose(xc, (0, 2, 1)))
        x_dbl = x @ x_proj_w.T
        dt, Bm, Cm = jnp.split(x_dbl, [DR, DR + DS], axis=-1)
        dt = jax.nn.softplus(dt @ dt_proj_w.T + dt_proj_b)
        A = -jnp.exp(A_log)

        def step(hstate, inp):
            dt_t, u_t, B_t, C_t = inp
            dA = jnp.exp(dt_t[..., None] * A)
            hstate = dA * hstate + (dt_t * u_t)[..., None] * B_t[:, None, :]
            y = jnp.einsum('bdn,bn->bd', hstate, C_t)
            return (hstate, y)
        batch = hidden_states.shape[0]
        h0 = jnp.zeros((batch, DI, DS), x.dtype)
        xs = (jnp.transpose(dt, (1, 0, 2)), jnp.transpose(x, (1, 0, 2)), jnp.transpose(Bm, (1, 0, 2)), jnp.transpose(Cm, (1, 0, 2)))
        _, ys = jax.lax.scan(step, h0, xs)
        y = jnp.transpose(ys, (1, 0, 2)) + x * D
        out = y * jax.nn.silu(z) @ out_proj_w.T + residual
        return out

    def _L0_ffn_ref(x, mix_kernel, W1, b1, W2, b2, Wo1, bo1, Wo2, bo2, gamma, beta):
        import jax, jax.numpy as jnp
        import numpy as np
        B, S, D = (4, 256, 128)
        P = 9
        DM = D // 4
        EPS = 1e-05

        def _mix(x, mix_kernel):
            xp = jnp.pad(x, ((0, 0), (1, 1), (0, 0)))
            return mix_kernel[0] * xp[:, :-2] + mix_kernel[1] * xp[:, 1:-1] + mix_kernel[2] * xp[:, 2:]

        def _layernorm(h, gamma, beta):
            mu = jnp.mean(h, axis=-1, keepdims=True)
            var = jnp.var(h, axis=-1, keepdims=True)
            return (h - mu) * jax.lax.rsqrt(var + EPS) * gamma + beta
        x_mixed = _mix(x, mix_kernel)
        h = jnp.einsum('bsd,pdm->bspm', x_mixed, W1) + b1
        stacked_paths = jnp.einsum('bspm,pmd->bspd', h, W2) + b2
        scores = jnp.tanh(x_mixed @ Wo1 + bo1) @ Wo2 + bo2
        idx = jnp.argmax(scores, axis=-1)
        weights = jax.nn.one_hot(idx, P, dtype=stacked_paths.dtype)
        collapsed = jnp.einsum('bspd,bsp->bsd', stacked_paths, weights)
        return _layernorm(x + collapsed, gamma, beta)
    x = L0_attn_hidden_states
    x = _layernorm(x + _L0_attn_ref(x, L0_attn_norm_w, L0_attn_norm_b, L0_attn_in_proj_w, L0_attn_conv_w, L0_attn_conv_b, L0_attn_x_proj_w, L0_attn_dt_proj_w, L0_attn_dt_proj_b, L0_attn_A_log, L0_attn_D, L0_attn_out_proj_w), axis=-1)
    x = _layernorm(x + _L0_ffn_ref(x, L0_ffn_mix_kernel, L0_ffn_W1, L0_ffn_b1, L0_ffn_W2, L0_ffn_b2, L0_ffn_Wo1, L0_ffn_bo1, L0_ffn_Wo2, L0_ffn_bo2, L0_ffn_gamma, L0_ffn_beta), axis=-1)
    return x

_drawn_inputs = setup_inputs


def setup_inputs(seed=0):
    import zlib

    import numpy as np

    out = dict(_drawn_inputs(seed))
    spreads = {'L0_attn_norm_w': (1.0, 0.6),
     'L0_attn_norm_b': (0.0, 0.8),
     'L0_attn_conv_b': (0.0, 0.589),
     'L0_attn_D': (1.0, 0.6),
     'L0_ffn_b1': (0.0, 0.1),
     'L0_ffn_b2': (0.0, 0.1),
     'L0_ffn_bo1': (0.0, 0.1),
     'L0_ffn_bo2': (0.0, 0.1),
     'L0_ffn_gamma': (1.0, 0.2),
     'L0_ffn_beta': (0.0, 0.1)}
    factors = {'L0_attn_in_proj_w': 6.419,
     'L0_attn_conv_w': 8.0,
     'L0_attn_x_proj_w': 8.0,
     'L0_attn_dt_proj_w': 8.0,
     'L0_attn_dt_proj_b': 8.0,
     'L0_attn_A_log': 8.0,
     'L0_attn_out_proj_w': 5.836}
    for name, (base, spread) in spreads.items():
        noise = np.random.default_rng([zlib.crc32(name.encode()), seed]).standard_normal(out[name].shape)
        drawn = base * np.exp(spread * noise) if base else spread * noise
        out[name] = jnp.asarray(drawn.astype(out[name].dtype))
    for name, factor in factors.items():
        out[name] = (out[name] * factor).astype(out[name].dtype)
    return out
```

```python
import numpy as np
import concourse.bass as bass
from concourse import mybir
from contextlib import ExitStack

f32 = mybir.dt.float32
bf16 = mybir.dt.bfloat16
ALU = mybir.AluOpType
ACT = mybir.ActivationFunctionType
AX = mybir.AxisListType

BATCH, SEQ, DM = 8, 1024, 128
DI, DS, DC, DR = 256, 16, 4, 64
PATHS, PW = 9, 32
P = 128
TILES = SEQ // P
HALF = SEQ // 2
TQ = HALF // P
BLK = DI // P
DG, DW = DI // 32, 32
NG = DS // 4
UNITS = 2 * DG
XR = 4
EPS = 1e-5
NA = 16
NB = 22
PRE_STEPS, POST_STEPS = 17, 34


def need(eng, sem, count):
    if not isinstance(count, int) or count > 0:
        eng.wait_ge(sem, count)


class Steps:

    def __init__(self, eng, sem, total):
        self.eng, self.sem, self.total, self.k, self.g = eng, sem, total, 0, 0

    def begin(self, g):
        self.g, self.k = g, 0

    def did(self, ins):
        self.k += 1
        ins.then_inc(self.sem, 1)

    def wait(self):
        need(self.eng, self.sem, self.g * self.total + self.k)

    def end(self):
        assert self.k == self.total, (self.k, self.total)


def build(nc, x_in, wxz_in, convw_in, convb_in, normw_in, normb_in, xpw_in, dtw_in, dtb_in, alog_in, dpar_in,
          wo_in, mix_in, w1_in, b1_in, w2_in, wo2_in, bo2_in, gamma_in, beta_in, ident_in, selrep_in,
          sel32_in, ssum_in, pathsel_in, desc_in, out):
    x_tok = x_in.rearrange("b (n p) m -> b p n m", p=P)
    out_tok = out.rearrange("b (n p) m -> b p n m", p=P)
    bc_dram = nc.dram_tensor("bc_rows", [2, 2, DS, SEQ], f32, kind="Internal").ap()

    with ExitStack() as ctx:
        def sb(name, shape, dt=f32):
            return ctx.enter_context(nc.sbuf_tensor(name, shape, dt))

        def ps(name, shape, dt=f32):
            return ctx.enter_context(nc.psum_tensor(name, shape, dt))

        def sem(name):
            return ctx.enter_context(nc.semaphore(name))

        wxz = sb("wxz", [P, 2 * DI])
        convw = sb("convw", [P, BLK, DC])
        convb = sb("convb", [P, BLK])
        normw = sb("normw", [P, 1])
        normb = sb("normb", [P, 1])
        xpw = sb("xpw", [P, BLK, DR + 2 * DS])
        dtw = sb("dtw", [DR + 2 * DS, DI])
        dtb = sb("dtb", [P, BLK])
        a_neg = sb("a_neg", [P, DG * NG])
        dpar = sb("dpar", [P, BLK])
        wo = sb("wo", [P, BLK, DM])
        mix = sb("mix", [P, 3])
        w1 = sb("w1", [P, PATHS * PW + PW])
        b1 = sb("b1", [P, 3])
        w2 = sb("w2", [P, 3, DM])
        wo2 = sb("wo2", [P, PATHS])
        bo2 = sb("bo2", [P, PATHS])
        gamma = sb("gamma", [P, DM])
        beta = sb("beta", [P, DM])
        ident = sb("ident", [P, P])
        selrep = sb("selrep", [P, 4, P])
        sel32 = sb("sel32", [P, 4, DW])
        seld = sb("seld", [P, BLK, 4, DW])
        ssum = sb("ssum", [P, DW])
        pathsel = sb("pathsel", [PATHS, 3, P], bf16)
        desc = sb("desc", [P, PATHS])

        xt = sb("xt", [P, TILES, DM])
        ht = sb("ht", [P, SEQ])
        xpad = sb("xpad", [P, DC - 1 + SEQ])
        sp_ln = sb("sp_ln", [P, SEQ])
        sp_t = sb("sp_t", [P, SEQ])
        xd = sb("xd", [DR + 2 * DS, SEQ])
        dtv = [sb(f"dtv{q}", [P, BLK, SEQ]) for q in range(2)]
        duv = [sb(f"duv{q}", [P, BLK, SEQ]) for q in range(2)]
        u = [sb(f"u{q}", [P, BLK, SEQ]) for q in range(2)]
        zs = sb("zs", [P, 2, DG, P])
        b_rep = [sb(f"b_rep{h}", [P, NG, HALF]) for h in range(2)]
        c_rep = [sb(f"c_rep{h}", [P, NG, HALF]) for h in range(2)]
        decay = sb("decay", [P, 2, NG, HALF])
        st = sb("st", [P, XR, NG, HALF])
        h_last = sb("h_last", [P, DG, NG])
        g = sb("g", [P, DG, P])
        g_blk = sb("g_blk", [P, BLK, TQ, P])
        s = sb("s", [P, TILES, DM])
        x1 = sb("x1", [P, TILES, DM])
        x1t = sb("x1t", [P, SEQ + 2])
        xm = sb("xm", [P, SEQ])
        hid = sb("hid", [P, 3, HALF])
        pathsel32 = xm[0:PATHS, 0:3 * P]
        oh_t = sb("oh_t", [PATHS, HALF], bf16)
        bn = [sb(f"bn{k}", [P, TILES, 6]) for k in range(2)]
        sm = [[sb(f"sm{k}_{i}", [P, TILES]) for i in range(8)] for k in range(2)]
        sc = [sb(f"sc{i}", [P, TQ, PATHS]) for i in range(3)]
        scm = [sb(f"scm{i}", [P, TQ]) for i in range(2)]

        dt_bank = [ps(f"dt_bank{i}", [P, HALF]) for i in range(2)]
        du_bank = [ps(f"du_bank{i}", [P, HALF]) for i in range(2)]
        y_bank = [ps(f"y_bank{i}", [P, 4 * P]) for i in range(2)]
        bank_a = ps("bank_a", [P, 512])
        bank_b = ps("bank_b", [P, 512])

        w_loaded = sem("w_loaded")
        tables_ready = sem("tables_ready")
        a_exp = sem("a_exp")
        x_loaded = sem("x_loaded")
        ln0_var = sem("ln0_var")
        ln0_log = sem("ln0_log")
        ln0_rough = sem("ln0_rough")
        ln0_done = sem("ln0_done")
        a_full = sem("a_full")
        a_free = sem("a_free")
        conv_done = sem("conv_done")
        u_ready = sem("u_ready")
        sp_abs = sem("sp_abs")
        sp_exp = sem("sp_exp")
        sp_log = sem("sp_log")
        sp_used = sem("sp_used")
        dt_ready = sem("dt_ready")
        bc_stored = sem("bc_stored")
        b_loaded = [sem(f"b_loaded{h}") for h in range(2)]
        c_loaded = [sem(f"c_loaded{h}") for h in range(2)]
        pre_step = sem("pre_step")
        post_step = sem("post_step")
        dt_rep_full = sem("dt_rep_full")
        du_rep_full = sem("du_rep_full")
        decay_done = sem("decay_done")
        dbu_done = sem("dbu_done")
        scan_done = sem("scan_done")
        h_saved = sem("h_saved")
        cmul_done = sem("cmul_done")
        ysum_done = sem("ysum_done")
        gate_done = sem("gate_done")
        g_moved = sem("g_moved")
        xr_loaded = sem("xr_loaded")
        b_full = sem("b_full")
        b_free = sem("b_free")
        ln_var = [None] + [sem(f"ln{k}_var") for k in (1, 2, 3)]
        ln_log = [None] + [sem(f"ln{k}_log") for k in (1, 2, 3)]
        ln_rough = [None] + [sem(f"ln{k}_rough") for k in (1, 2, 3)]
        ln1_done = sem("ln1_done")
        xmix_done = sem("xmix_done")
        oh_ready = sem("oh_ready")
        oh_copied = sem("oh_copied")
        s2_done = sem("s2_done")
        x1b_ready = sem("x1b_ready")
        out_ready = sem("out_ready")
        out_stored = sem("out_stored")

        LOADS = [(wxz, wxz_in), (convw, convw_in), (convb, convb_in), (normw, normw_in), (normb, normb_in),
                 (xpw, xpw_in), (dtw, dtw_in), (dtb, dtb_in), (a_neg, alog_in), (dpar, dpar_in), (wo, wo_in),
                 (mix, mix_in), (w1, w1_in), (b1, b1_in), (w2, w2_in), (wo2, wo2_in), (bo2, bo2_in),
                 (gamma, gamma_in), (beta, beta_in), (ident, ident_in), (selrep, selrep_in), (sel32, sel32_in),
                 (ssum, ssum_in), (desc, desc_in)]
        LOADED = 16 * (len(LOADS) + 1)

        block = ctx.enter_context(nc.Block())

        def program(eng, body):
            body(-1, 1, False, True, False)
            body(0, 0, True, True, False)
            with eng.Fori(0, (BATCH - 2) // 2) as pair:
                body(2 * pair + 1, 1, True, True, True)
                body(2 * pair + 2, 0, True, True, True)
            body(BATCH - 1, (BATCH - 1) % 2, True, False, True)
            body(BATCH, BATCH % 2, False, False, True)

        @block.sync
        def _(sp):
            def reached(sem, count):
                need(sp, sem, count)

            def load_bc(counts, q, h, loaded_by):
                for which, rep, sem_, used in ((0, b_rep, b_loaded, dbu_done), (1, c_rep, c_loaded, cmul_done)):
                    reached(used, counts[loaded_by])
                    for n in range(4):
                        rows = bc_dram[q, which].rearrange("(g n) t -> n g t", n=4)[n, :, h * HALF:(h + 1) * HALF]
                        sp.dma_start(rep[h][32 * n:32 * n + 32, :, :],
                                     rows.unsqueeze(0).broadcast_to([32, NG, HALF])).then_inc(sem_[h], 16)

            def reshuffle(gates, projected):
                reached(gate_done, gates)
                reached(b_full, projected)
                for tq in range(TQ):
                    for j in range(4):
                        sp.dma_start(g_blk[32 * j:32 * j + 32, :, tq, :],
                                     g[32 * tq:32 * tq + 32, :, :].rearrange("d (c j) t -> d j c t", j=4)[:, j]
                                     ).then_inc(g_moved, 16)

            for dst, src in LOADS:
                full = tuple(slice(None) for _ in dst.shape)
                sp.dma_start(dst[full], src).then_inc(w_loaded, 16)
            sp.dma_start(pathsel32, pathsel_in).then_inc(w_loaded, 16)

            def body(b, q, main, pre, post):
                counts = dict(transposed=NA * b + 2, half_read=UNITS * b, gates_before=4 * b, projected_0=NB * b - NB + 1,
                              xd_ready=NA * (b + 1) + 8, rows_read=64 * b, rows_stored=32 * (b + 2),
                              half_read_next=UNITS * b + DG, gates_0=4 * b + 2, projected_1=NB * b - NB + 2,
                              out_before=b, stored=16 * b)
                if not isinstance(b, int):
                    counts = {k: sp.to_reg(c) for k, c in counts.items()}
                for v in range(UNITS):
                    if v == 0 and pre:
                        reached(a_full, counts["transposed"])
                        sp.dma_start(xt[:, :, :], x_tok[b + 1]).then_inc(x_loaded, 16)
                    if v == 3 and main:
                        load_bc(counts, q, 1, "half_read")
                    if v == 3 and post:
                        reshuffle(counts["gates_before"], counts["projected_0"])
                    if v == 10 and pre:
                        reached(a_free, counts["xd_ready"])
                        reached(b_loaded[1], counts["rows_read"])
                        reached(c_loaded[1], counts["rows_read"])
                        for which in range(2):
                            sp.dma_start(bc_dram[1 - q, which], xd[DR + DS * which:DR + DS * which + DS, :]
                                         ).then_inc(bc_stored, 16)
                        reached(bc_stored, counts["rows_stored"])
                        load_bc(counts, 1 - q, 0, "half_read_next")
                    if v == 11 and main:
                        reshuffle(counts["gates_0"], counts["projected_1"])
                    if v == 14 and post:
                        reached(out_ready, counts["out_before"])
                        sp.dma_start(out_tok[b - 1], s[:, :, :]).then_inc(out_stored, 16)
                    if v == 14 and main:
                        reached(out_stored, counts["stored"])
                        sp.dma_start(s[:, :, :], x_tok[b]).then_inc(xr_loaded, 16)

            program(sp, body)
            sp.wait_ge(out_stored, 16 * BATCH)
            sp.wait_ge(bc_stored, 32 * BATCH)

        @block.tensor
        def _(pe):
            pe.wait_ge(w_loaded, LOADED)
            pe.wait_ge(tables_ready, 2)
            mm = nc.tensor.matmul

            def job_a(b, k):
                need(pe, a_free, NA * b + k)

            def job_b(b, k):
                need(pe, b_free, NB * b + k)

            def replicate(b, q, v):
                h, dg = v // DG, v % DG
                w = UNITS * b + v
                cols = slice(h * HALF, (h + 1) * HALF)
                if v == 0:
                    pe.wait_ge(dt_ready, 2 * (b + 1))
                need(pe, decay_done, NG * (w - 1))
                mm(dt_bank[v % 2][:, :], selrep[:, dg % 4, :], dtv[q][:, dg // 4, cols],
                   start=True, stop=True).then_inc(dt_rep_full, 1)
                need(pe, dbu_done, w - 1)
                mm(du_bank[v % 2][:, :], selrep[:, dg % 4, :], duv[q][:, dg // 4, cols],
                   start=True, stop=True).then_inc(du_rep_full, 1)

            def sum_states(b, q, v):
                h, dg = v // DG, v % DG
                k, col = dg // 4, (dg % 4) * P
                pe.wait_ge(cmul_done, UNITS * b + v + 1)
                if dg % 4 == 0:
                    need(pe, gate_done, 4 * b + 2 * h + k - 1)
                for n in range(NG + 1):
                    for tq in range(TQ):
                        o = y_bank[k][32 * tq:32 * tq + 32, col:col + P]
                        if n == 0:
                            t0 = h * HALF + tq * P
                            last = mm(o, seld[:, k, dg % 4, :], u[q][:, k, t0:t0 + P], start=True, stop=False)
                        else:
                            last = mm(o, ssum[:, :], st[:, v % XR, n - 1, tq * P:(tq + 1) * P],
                                      start=False, stop=n == NG)
                last.then_inc(ysum_done, 1)

            def body(b, q, main, pre, post):
                c = b + 1
                for v in range(UNITS):
                    if v < UNITS - 2 and main:
                        replicate(b, q, v + 2)
                    if v >= UNITS - 2 and pre:
                        replicate(c, 1 - q, v + 2 - UNITS)
                    if v >= 2 and main:
                        sum_states(b, q, v - 2)
                    if v < 2 and post:
                        sum_states(b - 1, 1 - q, v + UNITS - 2)
                    if v in (2, 3) and main:
                        for k in range(2):
                            h = v - 2
                            job_a(b, 12 + 2 * h + k)
                            if h == 0 and k == 0:
                                need(pe, a_free, NA * b + 2)
                            for j in range(4):
                                for tq in range(TQ):
                                    d0 = DI + (4 * k + j) * DW
                                    t0 = h * HALF + tq * P
                                    last = mm(bank_a[32 * tq:32 * tq + 32, j * P:(j + 1) * P], wxz[:, d0:d0 + DW],
                                              ht[:, t0:t0 + P], start=True, stop=True)
                            last.then_inc(a_full, 1)
                    if v == 4 and pre:
                        pe.wait_ge(ln0_done, c + 1)
                        for h in range(2):
                            job_a(c, h)
                            for t in range(TQ):
                                last = nc.tensor.transpose(bank_a[:, t * P:(t + 1) * P], xt[:, TQ * h + t, :],
                                                           ident[:, :])
                            last.then_inc(a_full, 1)
                    if v in (5, 7) and pre:
                        k = (v - 5) // 2
                        for h in range(2):
                            job_a(c, 2 + 2 * k + h)
                            mm(bank_a[:, :], wxz[:, k * P:(k + 1) * P], ht[:, h * HALF:(h + 1) * HALF],
                               start=True, stop=True).then_inc(a_full, 1)
                    if v == 9 and pre:
                        pe.wait_ge(u_ready, 2 * (c + 1))
                        for h in range(2):
                            job_a(c, 6 + h)
                            for k in range(BLK):
                                last = mm(bank_a[0:DR + 2 * DS, :], xpw[:, k, :],
                                          u[1 - q][:, k, h * HALF:(h + 1) * HALF], start=k == 0, stop=k == BLK - 1)
                            last.then_inc(a_full, 1)
                    if v in (10, 11) and pre:
                        k = v - 10
                        for h in range(2):
                            job_a(c, 8 + 2 * k + h)
                            mm(bank_a[:, :], dtw[:, k * P:(k + 1) * P], xd[:, h * HALF:(h + 1) * HALF],
                               start=True, stop=True).then_inc(a_full, 1)
                    o = b if v == 15 else b - 1
                    if (v == 15 and main) or (v == 4 and post):
                        h = 0 if v == 15 else 1
                        job_b(o, h)
                        pe.wait_ge(g_moved, 256 * (2 * o + h + 1))
                        for tq in range(TQ):
                            for k in range(BLK):
                                last = mm(bank_b[:, tq * DM:(tq + 1) * DM], g_blk[:, k, tq, :], wo[:, k, :],
                                          start=k == 0, stop=k == BLK - 1)
                        last.then_inc(b_full, 1)
                    if v == 6 and post:
                        pe.wait_ge(ln1_done, b)
                        for h in range(2):
                            job_b(b - 1, 2 + h)
                            for t in range(TQ):
                                last = nc.tensor.transpose(bank_b[:, t * P:(t + 1) * P], x1[:, TQ * h + t, :],
                                                           ident[:, :])
                            last.then_inc(b_full, 1)
                    if v in (8, 11) and post:
                        h = 0 if v == 8 else 1
                        base = 4 + 9 * h
                        cols = slice(h * HALF, (h + 1) * HALF)
                        pe.wait_ge(xmix_done, b)
                        for k in range(3):
                            m = P if k < 2 else 2 * PW
                            job_b(b - 1, base + k)
                            mm(bank_b[0:m, :], w1[:, k * P:k * P + m], xm[:, cols],
                               start=True, stop=True).then_inc(b_full, 1)
                        job_b(b - 1, base + 3)
                        for t in range(TQ):
                            last = mm(bank_b[:, t * PATHS:(t + 1) * PATHS], hid[:, 2, t * P:(t + 1) * P], wo2[:, :],
                                      start=True, stop=True)
                        last.then_inc(b_full, 1)
                    if v in (9, 12) and post:
                        h = 0 if v == 9 else 1
                        base = 4 + 9 * h
                        job_b(b - 1, base + 4)
                        pe.wait_ge(oh_ready, 2 * (b - 1) + h + 1)
                        for t in range(TQ):
                            last = nc.tensor.transpose(bank_b[0:PATHS, t * P:(t + 1) * P], sc[2][:, t, :], ident[:, :])
                        last.then_inc(b_full, 1)
                        for k in range(3):
                            job_b(b - 1, base + 5 + k)
                            mm(bank_b[:, :], pathsel[:, k, :], oh_t[:, :], start=True, stop=True).then_inc(b_full, 1)
                    if v in (10, 13) and post:
                        h = 0 if v == 10 else 1
                        job_b(b - 1, 4 + 9 * h + 8)
                        for t in range(TQ):
                            for k in range(3):
                                last = mm(bank_b[:, t * DM:(t + 1) * DM], hid[:, k, t * P:(t + 1) * P], w2[:, k, :],
                                          start=k == 0, stop=k == 2)
                        last.then_inc(b_full, 1)

            program(pe, body)

        @block.scalar
        def _(act):
            act.wait_ge(w_loaded, LOADED)
            nc.scalar.activation(a_neg[:, :], a_neg[:, :], ACT.Exp).then_inc(a_exp, 1)
            act.wait_ge(tables_ready, 2)

            def rough_rsqrt(g_, buf, var, log, rough):
                act.wait_ge(var, g_ + 1)
                nc.scalar.activation(sm[buf][5][:, :], sm[buf][4][:, :], ACT.Ln).then_inc(log, 1)
                act.wait_ge(log, g_ + 1)
                nc.scalar.activation(sm[buf][6][:, :], sm[buf][5][:, :], ACT.Exp, scale=-0.5).then_inc(rough, 1)

            def decays(b, v):
                w = UNITS * b + v
                act.wait_ge(dt_rep_full, w + 1)
                need(act, scan_done, NG * (w - 1))
                for n in range(NG):
                    k = (v % DG) * NG + n
                    nc.scalar.activation(decay[:, v % 2, n, :], dt_bank[v % 2][:, :], ACT.Exp,
                                         scale=a_neg[:, k:k + 1]).then_inc(decay_done, 1)

            def body(b, q, main, pre, post):
                c = b + 1
                for v in range(UNITS):
                    if v < UNITS - 1 and main:
                        decays(b, v + 1)
                    if v == UNITS - 1 and pre:
                        decays(c, 0)
                    if v in (2, 3) and main:
                        h = v - 2
                        for k in range(2):
                            act.wait_ge(a_full, NA * b + 12 + 2 * h + k + 1)
                            need(act, gate_done, 4 * b)
                            nc.scalar.activation(zs[:, h, 4 * k:4 * k + 4, :],
                                                 bank_a[:, :].rearrange("p (j t) -> p j t", j=4), ACT.Silu
                                                 ).then_inc(a_free, 1)
                    if v == 3 and pre:
                        rough_rsqrt(c, 0, ln0_var, ln0_log, ln0_rough)
                    if v == 4 and pre:
                        for h in range(2):
                            act.wait_ge(a_full, NA * c + h + 1)
                            nc.scalar.activation(ht[:, h * HALF:(h + 1) * HALF], bank_a[:, :], ACT.Identity,
                                                 scale=normw[:, 0:1], bias=normb[:, 0:1]).then_inc(a_free, 1)
                    if v in (5, 7) and pre:
                        k = (v - 5) // 2
                        need(act, conv_done, 2 * c + k)
                        for h in range(2):
                            act.wait_ge(a_full, NA * c + 2 + 2 * k + h + 1)
                            nc.scalar.activation(xpad[:, DC - 1 + h * HALF:DC - 1 + (h + 1) * HALF], bank_a[:, :],
                                                 ACT.Copy).then_inc(a_free, 1)
                    if v == 9 and pre:
                        for k in range(BLK):
                            act.wait_ge(conv_done, 2 * c + k + 1)
                            nc.scalar.activation(u[1 - q][:, k, :], u[1 - q][:, k, :], ACT.Silu).then_inc(u_ready, 1)
                    if v == 9 and pre:
                        need(act, bc_stored, 32 * (b + 1))
                        for h in range(2):
                            act.wait_ge(a_full, NA * c + 6 + h + 1)
                            nc.scalar.activation(xd[:, h * HALF:(h + 1) * HALF], bank_a[0:DR + 2 * DS, :], ACT.Copy
                                                 ).then_inc(a_free, 1)
                    if v in (10, 11) and pre:
                        k = v - 10
                        for h in range(2):
                            cols = slice(h * HALF, (h + 1) * HALF)
                            act.wait_ge(a_full, NA * c + 8 + 2 * k + h + 1)
                            nc.scalar.activation(duv[1 - q][:, k, cols], bank_a[:, :], ACT.Abs,
                                                 bias=dtb[:, k:k + 1]).then_inc(sp_abs, 1)
                            nc.scalar.activation(dtv[1 - q][:, k, cols], bank_a[:, :], ACT.Relu,
                                                 bias=dtb[:, k:k + 1]).then_inc(a_free, 1)
                        act.wait_ge(sp_abs, 4 * c + 2 * k + 2)
                        nc.scalar.activation(duv[1 - q][:, k, :], duv[1 - q][:, k, :], ACT.Exp, scale=-1.0
                                             ).then_inc(sp_exp, 1)
                        act.wait_ge(sp_exp, 2 * c + k + 1)
                        need(act, sp_used, 2 * c + k)
                        nc.scalar.activation(sp_ln[:, :], duv[1 - q][:, k, :], ACT.Ln, bias=1.0).then_inc(sp_log, 1)
                    if v == 5 and post:
                        rough_rsqrt(b - 1, 1, ln_var[1], ln_log[1], ln_rough[1])
                    if v == 6 and post:
                        for h in range(2):
                            act.wait_ge(b_full, NB * (b - 1) + 2 + h + 1)
                            nc.scalar.activation(x1t[:, 1 + h * HALF:1 + (h + 1) * HALF], bank_b[:, :], ACT.Copy
                                                 ).then_inc(b_free, 1)
                    if v in (8, 11) and post:
                        base = NB * (b - 1) + (4 if v == 8 else 13)
                        for k in range(3):
                            act.wait_ge(b_full, base + k + 1)
                            if k < 2:
                                nc.scalar.activation(hid[:, k, :], bank_b[:, :], ACT.Identity, bias=b1[:, k:k + 1]
                                                     ).then_inc(b_free, 1)
                            else:
                                nc.scalar.activation(hid[0:PW, k, :], bank_b[0:PW, :], ACT.Identity,
                                                     bias=b1[0:PW, k:k + 1])
                                nc.scalar.activation(hid[PW:2 * PW, k, :], bank_b[PW:2 * PW, :], ACT.Tanh,
                                                     bias=b1[PW:2 * PW, k:k + 1]).then_inc(b_free, 1)
                    if v in (9, 12) and post:
                        base = NB * (b - 1) + (4 if v == 9 else 13)
                        act.wait_ge(b_full, base + 5)
                        nc.scalar.activation(oh_t[:, :], bank_b[0:PATHS, :], ACT.Copy).then_inc(oh_copied, 1)
                        nc.scalar.activation(hid[PW:PW + PATHS, 2, :], bank_b[0:PATHS, :], ACT.Copy).then_inc(b_free, 1)
                    if v == 14 and post:
                        rough_rsqrt(b - 1, 1, ln_var[2], ln_log[2], ln_rough[2])
                        rough_rsqrt(b - 1, 1, ln_var[3], ln_log[3], ln_rough[3])

            program(act, body)

        @block.gpsimd
        def _(pool):
            def body(b, q, main, pre, post):
                for v in range(UNITS):
                    if main:
                        h, dg, w = v // DG, v % DG, UNITS * b + v
                        pool.wait_ge(scan_done, NG * w + NG)
                        if h == 0:
                            pool.wait_ge(h_saved, DG * b + dg + 1)
                        if dg == 0:
                            pool.wait_ge(c_loaded[h], 64 * (b + 1))
                        nc.gpsimd.tensor_tensor(st[:, v % XR, :, :], st[:, v % XR, :, :], c_rep[h][:, :, :], ALU.mult
                                                ).then_inc(cmul_done, 1)
                    if v == 13 and post:
                        if not main:
                            pool.wait_ge(w_loaded, LOADED)
                        pool.wait_ge(s2_done, b)
                        nc.gpsimd.tensor_tensor(x1[:, :, :], x1[:, :, :],
                                                beta[:, :].unsqueeze(1).broadcast_to([P, TILES, DM]), ALU.add
                                                ).then_inc(x1b_ready, 1)

            pool.wait_ge(w_loaded, LOADED)
            program(pool, body)

        @block.vector
        def _(dve):
            tt, ts, stt = nc.vector.tensor_tensor, nc.vector.tensor_scalar, nc.vector.scalar_tensor_tensor
            before = Steps(dve, pre_step, PRE_STEPS)
            after = Steps(dve, post_step, POST_STEPS)

            nc.vector.memset(xpad[:, 0:DC - 1], 0.0)
            nc.vector.memset(x1t[:, 0:1], 0.0)
            nc.vector.memset(x1t[:, SEQ + 1:SEQ + 2], 0.0)
            nc.vector.memset(hid[:, 2, :], 0.0).then_inc(tables_ready, 1)
            dve.wait_ge(w_loaded, LOADED)
            dve.wait_ge(a_exp, 1)
            ts(a_neg[:, :], a_neg[:, :], -1.0, None, ALU.mult)
            nc.vector.tensor_copy(pathsel[:, :, :], pathsel32.rearrange("p (k n) -> p k n", k=3))
            for k in range(BLK):
                last = ts(seld[:, k, :, :], sel32[:, :, :], dpar[:, k:k + 1], None, ALU.mult)
            last.then_inc(tables_ready, 1)
            dve.wait_ge(tables_ready, 2)

            def statistics(steps, buf, src):
                mean, diff, var2, _, veps = sm[buf][0:5]
                for t in range(TILES):
                    last = nc.vector.bn_stats(bn[buf][:, t, :], src[:, t, :])
                steps.did(last)
                steps.wait()
                tt(mean[:, :], bn[buf][:, :, 1], bn[buf][:, :, 4], ALU.add)
                tt(diff[:, :], bn[buf][:, :, 1], bn[buf][:, :, 4], ALU.subtract)
                steps.did(tt(var2[:, :], bn[buf][:, :, 2], bn[buf][:, :, 5], ALU.add))
                steps.wait()
                ts(mean[:, :], mean[:, :], 0.5, None, ALU.mult)
                ts(var2[:, :], var2[:, :], 1.0 / DM, EPS, ALU.mult, ALU.add)
                steps.did(stt(diff[:, :], diff[:, :], 0.25, diff[:, :], ALU.mult, ALU.mult))
                steps.wait()
                return tt(veps[:, :], diff[:, :], var2[:, :], ALU.add)

            def refine(steps, buf):
                _, q_, _, _, veps, _, r0, r = sm[buf]
                steps.did(tt(q_[:, :], r0[:, :], r0[:, :], ALU.mult))
                steps.wait()
                steps.did(tt(q_[:, :], q_[:, :], veps[:, :], ALU.mult))
                steps.wait()
                steps.did(ts(q_[:, :], q_[:, :], -0.5, 1.5, ALU.mult, ALU.add))
                steps.wait()
                steps.did(tt(r[:, :], r0[:, :], q_[:, :], ALU.mult))
                steps.wait()

            def normalise(buf, dst, src):
                mean, r = sm[buf][0], sm[buf][7]
                for t in range(TILES):
                    last = ts(dst[:, t, :], src[:, t, :], mean[:, t:t + 1], r[:, t:t + 1], ALU.subtract, ALU.mult)
                return last

            def body(b, q, main, pre, post):
                c = b + 1
                for v in range(UNITS):
                    if main:
                        h, dg, w, r = v // DG, v % DG, UNITS * b + v, v % XR
                        dve.wait_ge(du_rep_full, w + 1)
                        need(dve, ysum_done, w - XR + 1)
                        if dg == 0:
                            dve.wait_ge(b_loaded[h], 64 * (b + 1))
                        tt(st[:, r, :, :], du_bank[v % 2][:, :].unsqueeze(1).broadcast_to([P, NG, HALF]),
                           b_rep[h][:, :, :], ALU.mult).then_inc(dbu_done, 1)
                        dve.wait_ge(dbu_done, w + 1)
                        if h == 1:
                            dve.wait_ge(h_saved, DG * b + dg + 1)
                        for n in range(NG):
                            dve.wait_ge(decay_done, NG * w + n + 1)
                            nc.vector.tensor_tensor_scan(st[:, r, n, :], decay[:, v % 2, n, :], st[:, r, n, :],
                                                         h_last[:, dg, n:n + 1] if h else 0.0,
                                                         ALU.mult, ALU.add).then_inc(scan_done, 1)
                        if h == 0:
                            dve.wait_ge(scan_done, NG * w + NG)
                            nc.vector.tensor_copy(h_last[:, dg, :], st[:, r, :, HALF - 1]).then_inc(h_saved, 1)

                    gates = {6: (b, 0, 0), 10: (b, 0, 1), 14: (b, 1, 0), 2: (b - 1, 1, 1)}
                    if v in gates and (post if v == 2 else main):
                        o, gh, k = gates[v]
                        dve.wait_ge(ysum_done, UNITS * o + DG * gh + 4 * k + 4)
                        dve.wait_ge(a_free, NA * o + 16)
                        need(dve, g_moved, 256 * (2 * o + gh))
                        tt(g[:, 4 * k:4 * k + 4, :], y_bank[k][:, :].rearrange("p (j t) -> p j t", j=4),
                           zs[:, gh, 4 * k:4 * k + 4, :], ALU.mult).then_inc(gate_done, 1)

                    if v == 2 and pre:
                        before.begin(c)
                        dve.wait_ge(x_loaded, 16 * (c + 1))
                        statistics(before, 0, xt).then_inc(ln0_var, 1)
                    if v == 3 and pre:
                        dve.wait_ge(ln0_var, c + 1)
                        dve.wait_ge(ln0_rough, c + 1)
                        refine(before, 0)
                        normalise(0, xt, xt).then_inc(ln0_done, 1)
                    if v in (6, 8) and pre:
                        k = (v - 6) // 2
                        dve.wait_ge(a_free, NA * c + 4 + 2 * k)
                        dst = u[1 - q][:, k, :]
                        before.did(ts(dst, xpad[:, 0:SEQ], convw[:, k, 0:1], convb[:, k:k + 1], ALU.mult, ALU.add))
                        for i in (1, 2):
                            before.wait()
                            before.did(stt(dst, xpad[:, i:i + SEQ], convw[:, k, i:i + 1], dst, ALU.mult, ALU.add))
                        before.wait()
                        stt(dst, xpad[:, 3:3 + SEQ], convw[:, k, 3:4], dst, ALU.mult, ALU.add).then_inc(conv_done, 1)
                    if v in (11, 12) and pre:
                        k = v - 11
                        y = duv[1 - q][:, k, :]
                        dtk = dtv[1 - q][:, k, :]
                        dve.wait_ge(sp_exp, 2 * c + k + 1)
                        ts(sp_t[:, :], y, 1.0, 1.0, ALU.add, ALU.subtract)
                        dve.wait_ge(sp_log, 2 * c + k + 1)
                        before.did(tt(dtk, dtk, sp_ln[:, :], ALU.add))
                        before.wait()
                        before.did(tt(y, y, sp_t[:, :], ALU.subtract))
                        before.wait()
                        tt(dtk, dtk, y, ALU.add).then_inc(sp_used, 1)
                        dve.wait_ge(sp_used, 2 * c + k + 1)
                        tt(y, dtk, u[1 - q][:, k, :], ALU.mult).then_inc(dt_ready, 1)
                    if v == 12 and pre:
                        dve.wait_ge(dt_ready, 2 * (c + 1))
                        before.end()

                    o = b if v == 15 else b - 1
                    if (v == 15 and main) or (v == 4 and post):
                        h = 0 if v == 15 else 1
                        if h == 0:
                            dve.wait_ge(xr_loaded, 16 * (o + 1))
                        dve.wait_ge(b_full, NB * o + h + 1)
                        sh = s[:, TQ * h:TQ * h + TQ, :]
                        stt(sh, sh, 2.0, bank_b[:, :].rearrange("p (t m) -> p t m", t=TQ), ALU.mult, ALU.add
                            ).then_inc(b_free, 1)
                    if v == 4 and post:
                        after.begin(b - 1)
                        dve.wait_ge(b_free, NB * (b - 1) + 2)
                        statistics(after, 1, s).then_inc(ln_var[1], 1)
                    if v == 5 and post:
                        dve.wait_ge(ln_rough[1], b)
                        refine(after, 1)
                        normalise(1, x1, s).then_inc(ln1_done, 1)
                    if v == 7 and post:
                        dve.wait_ge(b_free, NB * (b - 1) + 4)
                        after.did(ts(xm[:, :], x1t[:, 0:SEQ], mix[:, 0:1], None, ALU.mult))
                        after.wait()
                        after.did(stt(xm[:, :], x1t[:, 1:1 + SEQ], mix[:, 1:2], xm[:, :], ALU.mult, ALU.add))
                        after.wait()
                        stt(xm[:, :], x1t[:, 2:2 + SEQ], mix[:, 2:3], xm[:, :], ALU.mult, ALU.add).then_inc(xmix_done, 1)
                    if v in (8, 11) and post:
                        base = NB * (b - 1) + (4 if v == 8 else 13)
                        hh = 0 if v == 8 else 1
                        wide = [P, TQ, PATHS]
                        dve.wait_ge(b_full, base + 4)
                        tt(sc[0][:, :, :], bank_b[:, 0:TQ * PATHS].rearrange("p (t n) -> p t n", t=TQ),
                           bo2[:, :].unsqueeze(1).broadcast_to(wide), ALU.add).then_inc(b_free, 1)
                        dve.wait_ge(b_free, base + 4)
                        after.did(nc.vector.tensor_reduce(scm[0][:, :], sc[0][:, :, :], AX.X, ALU.max))
                        after.wait()
                        after.did(tt(sc[1][:, :, :], sc[0][:, :, :], scm[0][:, :].unsqueeze(2).broadcast_to(wide),
                                     ALU.is_equal))
                        after.wait()
                        after.did(tt(sc[1][:, :, :], sc[1][:, :, :], desc[:, :].unsqueeze(1).broadcast_to(wide),
                                     ALU.mult))
                        after.wait()
                        after.did(nc.vector.tensor_reduce(scm[1][:, :], sc[1][:, :, :], AX.X, ALU.max))
                        after.wait()
                        tt(sc[2][:, :, :], sc[1][:, :, :], scm[1][:, :].unsqueeze(2).broadcast_to(wide),
                           ALU.is_equal).then_inc(oh_ready, 1)
                    if v in (9, 12) and post:
                        base = NB * (b - 1) + (4 if v == 9 else 13)
                        for k in range(3):
                            m = P if k < 2 else PW
                            dve.wait_ge(b_full, base + 5 + k + 1)
                            tt(hid[0:m, k, :], hid[0:m, k, :], bank_b[0:m, :], ALU.mult).then_inc(b_free, 1)
                    if v in (10, 13) and post:
                        hh = 0 if v == 10 else 1
                        base = NB * (b - 1) + (4 if v == 10 else 13)
                        dve.wait_ge(b_full, base + 9)
                        i = tt(s[:, TQ * hh:TQ * hh + TQ, :], x1[:, TQ * hh:TQ * hh + TQ, :],
                               bank_b[:, :].rearrange("p (t m) -> p t m", t=TQ), ALU.add)
                        i.then_inc(b_free, 1)
                    if v == 13 and post:
                        dve.wait_ge(b_free, NB * b)
                        statistics(after, 1, s).then_inc(ln_var[2], 1)
                        dve.wait_ge(ln_var[2], b)
                        nc.vector.memset(sm[1][3][:, 0:1], 0.0).then_inc(s2_done, 1)
                    if v == 14 and post:
                        dve.wait_ge(ln_rough[2], b)
                        refine(after, 1)
                        after.did(normalise(1, s, s))
                        after.wait()
                        after.did(tt(s[:, :, :], s[:, :, :], gamma[:, :].unsqueeze(1).broadcast_to([P, TILES, DM]),
                                     ALU.mult))
                        after.wait()
                        dve.wait_ge(x1b_ready, b)
                        after.did(tt(s[:, :, :], s[:, :, :], x1[:, :, :], ALU.add))
                        after.wait()
                        statistics(after, 1, s).then_inc(ln_var[3], 1)
                        dve.wait_ge(ln_rough[3], b)
                        refine(after, 1)
                        normalise(1, s, s).then_inc(out_ready, 1)
                        after.end()

            program(dve, body)


def kernel(**inputs):
    import numpy as _np
    import concourse.bacc as _bacc
    from concourse import mybir as _mybir
    from concourse.bass_utils import run_bass_kernel_spmd as _run

    A = {k.replace("L0_", ""): _np.ascontiguousarray(v) for k, v in inputs.items()}
    F = _np.float32

    def blocks(v):
        return v.reshape((2, 128) + v.shape[1:]).swapaxes(0, 1)

    w1 = _np.zeros((128, 320), F)
    w1[:, 0:288] = A["ffn_W1"].transpose(1, 0, 2).reshape(128, 288)
    w1[:, 288:320] = A["ffn_Wo1"]
    b1 = _np.zeros((384,), F)
    b1[0:288] = A["ffn_b1"].reshape(288)
    b1[288:320] = A["ffn_bo1"]
    w2 = _np.zeros((384, 128), F)
    w2[0:288] = A["ffn_W2"].reshape(288, 128)
    w2[288:297] = A["ffn_b2"]
    wo2 = _np.zeros((128, 9), F)
    wo2[32:64] = A["ffn_Wo2"]
    dtw = _np.zeros((96, 256), F)
    dtw[0:64] = A["attn_dt_proj_w"].T
    selrep = _np.zeros((128, 4, 4, 32), F)
    sel32 = _np.zeros((128, 4, 32), F)
    ssum = _np.zeros((4, 32, 32), F)
    pathsel = _np.zeros((9, 384), F)
    for j in range(4):
        for d in range(32):
            selrep[32 * j + d, j, :, d] = 1
            sel32[32 * j + d, j, d] = 1
            ssum[j, d, d] = 1
    for p in range(9):
        pathsel[p, 32 * p:32 * p + 32] = 1
    arrays = [
        ("x", A["attn_hidden_states"]),
        ("wxz", A["attn_in_proj_w"].T),
        ("convw", blocks(A["attn_conv_w"][:, 0, :])),
        ("convb", blocks(A["attn_conv_b"])),
        ("normw", A["attn_norm_w"].reshape(128, 1)),
        ("normb", A["attn_norm_b"].reshape(128, 1)),
        ("xpw", blocks(A["attn_x_proj_w"].T)),
        ("dtw", dtw),
        ("dtb", blocks(A["attn_dt_proj_b"])),
        ("alog", A["attn_A_log"].reshape(8, 32, 4, 4).transpose(3, 1, 0, 2).reshape(128, 32)),
        ("dpar", blocks(A["attn_D"])),
        ("wo", blocks(A["attn_out_proj_w"].T)),
        ("mix", A["ffn_mix_kernel"].T),
        ("w1", w1),
        ("b1", b1.reshape(3, 128).T),
        ("w2", w2.reshape(3, 128, 128).transpose(1, 0, 2)),
        ("wo2", wo2),
        ("bo2", _np.broadcast_to(A["ffn_bo2"], (128, 9))),
        ("gamma", _np.broadcast_to(A["ffn_gamma"], (128, 128))),
        ("beta", _np.broadcast_to(A["ffn_beta"], (128, 128))),
        ("ident", _np.eye(128, dtype=F)),
        ("selrep", selrep.reshape(128, 4, 128)),
        ("sel32", sel32),
        ("ssum", ssum.reshape(128, 32)),
        ("pathsel", pathsel),
        ("desc", _np.broadcast_to(_np.arange(9, 0, -1).astype(F), (128, 9))),
    ]
    nc = _bacc.Bacc("TRN2", target_bir_lowering=False, num_devices=1)
    feeds, args = {}, []
    for name, a in arrays:
        a = _np.ascontiguousarray(a)
        feeds[f"in_{name}"] = a
        args.append(nc.dram_tensor(f"in_{name}", a.shape, _mybir.dt.float32, kind="ExternalInput").ap())
    args.append(nc.dram_tensor("out_y", (8, 1024, 128), _mybir.dt.float32, kind="ExternalOutput").ap())
    build(nc, *args)
    r = _run(nc, [feeds], core_ids=[0])
    return r.results[0]["out_y"]
```

```python
import numpy as np
import concourse.bass as bass
from concourse import mybir
from contextlib import ExitStack

f32 = mybir.dt.float32
bf16 = mybir.dt.bfloat16
ALU = mybir.AluOpType
ACT = mybir.ActivationFunctionType
AX = mybir.AxisListType

BATCH, SEQ, DM = 8, 1024, 128
DI, DS, DC, DR = 256, 16, 4, 64
PATHS, PW = 9, 32
P = 128
TILES = SEQ // P
HALF = SEQ // 2
TQ = HALF // P
BLK = DI // P
DG, DW = DI // 32, 32
NG = DS // 4
UNITS = 2 * DG
XR = 4
EPS = 1e-5
NA = 16
NB = 22
PRE_STEPS, POST_STEPS = 13, 34


def need(eng, sem, count):
    if not isinstance(count, int) or count > 0:
        eng.wait_ge(sem, count)


class Steps:

    def __init__(self, eng, sem, total):
        self.eng, self.sem, self.total, self.k, self.g = eng, sem, total, 0, 0

    def begin(self, g):
        self.g, self.k = g, 0

    def did(self, ins):
        self.k += 1
        ins.then_inc(self.sem, 1)

    def wait(self):
        need(self.eng, self.sem, self.g * self.total + self.k)

    def end(self):
        assert self.k == self.total, (self.k, self.total)


def build(nc, x_in, wxz_in, convw_in, convb_in, normw_in, normb_in, xpw_in, dtw_in, dtb_in, alog_in, dpar_in,
          wo_in, mix_in, w1_in, b1_in, w2_in, wo2_in, bo2_in, gamma_in, beta_in, ident_in, selrep_in,
          sel32_in, ssum_in, pathsel_in, desc_in, out):
    x_tok = x_in.rearrange("b (n p) m -> b p n m", p=P)
    out_tok = out.rearrange("b (n p) m -> b p n m", p=P)
    bc_dram = nc.dram_tensor("bc_rows", [2, 2, DS, SEQ], f32, kind="Internal").ap()

    with ExitStack() as ctx:
        def sb(name, shape, dt=f32):
            return ctx.enter_context(nc.sbuf_tensor(name, shape, dt))

        def ps(name, shape, dt=f32):
            return ctx.enter_context(nc.psum_tensor(name, shape, dt))

        def sem(name):
            return ctx.enter_context(nc.semaphore(name))

        wxz = sb("wxz", [P, 2 * DI])
        convw = sb("convw", [P, BLK, DC])
        convb = sb("convb", [P, BLK])
        normw = sb("normw", [P, 1])
        normb = sb("normb", [P, 1])
        xpw = sb("xpw", [P, BLK, DR + 2 * DS])
        dtw = sb("dtw", [DR + 2 * DS, DI])
        dtb = sb("dtb", [P, BLK])
        a_neg = sb("a_neg", [P, DG * NG])
        dpar = sb("dpar", [P, BLK])
        wo = sb("wo", [P, BLK, DM])
        mix = sb("mix", [P, 3])
        w1 = sb("w1", [P, PATHS * PW + PW])
        b1 = sb("b1", [P, 3])
        w2 = sb("w2", [P, 3, DM])
        wo2 = sb("wo2", [P, PATHS])
        bo2 = sb("bo2", [P, PATHS])
        gamma = sb("gamma", [P, DM])
        beta = sb("beta", [P, DM])
        ident = sb("ident", [P, P])
        selrep = sb("selrep", [P, 4, P])
        sel32 = sb("sel32", [P, 4, DW])
        seld = sb("seld", [P, BLK, 4, DW])
        ssum = sb("ssum", [P, DW])
        pathsel = sb("pathsel", [PATHS, 3, P], bf16)
        desc = sb("desc", [P, PATHS])

        xt = sb("xt", [P, TILES, DM])
        ht = sb("ht", [P, SEQ])
        xpad = sb("xpad", [P, DC - 1 + SEQ])
        sp_ln = sb("sp_ln", [P, SEQ])
        sp_t = sb("sp_t", [P, SEQ])
        xd = sb("xd", [DR + 2 * DS, SEQ])
        dtv = [sb(f"dtv{q}", [P, BLK, SEQ]) for q in range(2)]
        duv = [sb(f"duv{q}", [P, BLK, SEQ]) for q in range(2)]
        u = [sb(f"u{q}", [P, BLK, SEQ]) for q in range(2)]
        zs = sb("zs", [P, 2, DG, P])
        b_rep = [sb(f"b_rep{h}", [P, NG, HALF]) for h in range(2)]
        c_rep = [sb(f"c_rep{h}", [P, NG, HALF]) for h in range(2)]
        decay = sb("decay", [P, 2, NG, HALF])
        st = sb("st", [P, XR, NG, HALF])
        h_last = sb("h_last", [P, DG, NG])
        g = sb("g", [P, DG, P])
        g_blk = sb("g_blk", [P, BLK, TQ, P])
        s = sb("s", [P, TILES, DM])
        x1 = sb("x1", [P, TILES, DM])
        x1t = sb("x1t", [P, SEQ + 2])
        xm = sb("xm", [P, SEQ])
        hid = sb("hid", [P, 3, HALF])
        pathsel32 = xm[0:PATHS, 0:3 * P]
        oh_t = sb("oh_t", [PATHS, HALF], bf16)
        bn = [sb(f"bn{k}", [P, TILES, 6]) for k in range(2)]
        sm = [[sb(f"sm{k}_{i}", [P, TILES]) for i in range(8)] for k in range(2)]
        sc = [sb(f"sc{i}", [P, TQ, PATHS]) for i in range(3)]
        scm = [sb(f"scm{i}", [P, TQ]) for i in range(2)]

        dt_bank = ps("dt_bank", [P, HALF])
        du_bank = [ps(f"du_bank{i}", [P, HALF]) for i in range(2)]
        y_bank = [ps(f"y_bank{i}", [P, 4 * P]) for i in range(2)]
        bank_a = ps("bank_a", [P, 512])
        banks_b = [ps(f"bank_b{i}", [P, 512]) for i in range(2)]

        w_loaded = sem("w_loaded")
        tables_ready = sem("tables_ready")
        a_exp = sem("a_exp")
        x_loaded = sem("x_loaded")
        ln0_var = sem("ln0_var")
        ln0_log = sem("ln0_log")
        ln0_rough = sem("ln0_rough")
        ln0_done = sem("ln0_done")
        a_full = sem("a_full")
        a_free = sem("a_free")
        conv_done = sem("conv_done")
        u_ready = sem("u_ready")
        sp_abs = sem("sp_abs")
        sp_exp = sem("sp_exp")
        sp_log = sem("sp_log")
        sp_round = sem("sp_round")
        sp_small = sem("sp_small")
        sp_big = sem("sp_big")
        sp_sum = sem("sp_sum")
        dt_ready = sem("dt_ready")
        bc_stored = sem("bc_stored")
        b_loaded = [sem(f"b_loaded{h}") for h in range(2)]
        c_loaded = [sem(f"c_loaded{h}") for h in range(2)]
        pre_step = sem("pre_step")
        post_step = sem("post_step")
        dt_rep_full = sem("dt_rep_full")
        du_rep_full = sem("du_rep_full")
        decay_done = sem("decay_done")
        dbu_done = sem("dbu_done")
        scan_done = sem("scan_done")
        h_saved = sem("h_saved")
        cmul_done = sem("cmul_done")
        ysum_done = sem("ysum_done")
        gate_done = sem("gate_done")
        g_moved = sem("g_moved")
        xr_loaded = sem("xr_loaded")
        b_full = sem("b_full")
        b_free = [sem(f"b_free{i}") for i in range(2)]
        ln_var = [None] + [sem(f"ln{k}_var") for k in (1, 2, 3)]
        ln_log = [None] + [sem(f"ln{k}_log") for k in (1, 2, 3)]
        ln_rough = [None] + [sem(f"ln{k}_rough") for k in (1, 2, 3)]
        ln1_done = sem("ln1_done")
        xmix_done = sem("xmix_done")
        oh_ready = sem("oh_ready")
        oh_copied = sem("oh_copied")
        x1b_ready = sem("x1b_ready")
        out_ready = sem("out_ready")
        out_stored = sem("out_stored")

        LOADS = [(wxz, wxz_in), (convw, convw_in), (convb, convb_in), (normw, normw_in), (normb, normb_in),
                 (xpw, xpw_in), (dtw, dtw_in), (dtb, dtb_in), (a_neg, alog_in), (dpar, dpar_in), (wo, wo_in),
                 (mix, mix_in), (w1, w1_in), (b1, b1_in), (w2, w2_in), (wo2, wo2_in), (bo2, bo2_in),
                 (gamma, gamma_in), (beta, beta_in), (ident, ident_in), (selrep, selrep_in), (sel32, sel32_in),
                 (ssum, ssum_in), (desc, desc_in)]
        LOADED = 16 * (len(LOADS) + 1)

        block = ctx.enter_context(nc.Block())

        def program(eng, body):
            body(-1, 1, False, True, False)
            body(0, 0, True, True, False)
            with eng.Fori(0, (BATCH - 2) // 2) as pair:
                body(2 * pair + 1, 1, True, True, True)
                body(2 * pair + 2, 0, True, True, True)
            body(BATCH - 1, (BATCH - 1) % 2, True, False, True)
            body(BATCH, BATCH % 2, False, False, True)

        @block.sync
        def _(sp):
            def reached(sem, count):
                need(sp, sem, count)

            def load_bc(counts, q, h, loaded_by):
                for which, rep, sem_, used in ((0, b_rep, b_loaded, dbu_done), (1, c_rep, c_loaded, cmul_done)):
                    reached(used, counts[loaded_by])
                    for n in range(4):
                        rows = bc_dram[q, which].rearrange("(g n) t -> n g t", n=4)[n, :, h * HALF:(h + 1) * HALF]
                        sp.dma_start(rep[h][32 * n:32 * n + 32, :, :],
                                     rows.unsqueeze(0).broadcast_to([32, NG, HALF])).then_inc(sem_[h], 16)

            def reshuffle(gates, projected):
                reached(gate_done, gates)
                reached(b_full, projected)
                for tq in range(TQ):
                    for j in range(4):
                        sp.dma_start(g_blk[32 * j:32 * j + 32, :, tq, :],
                                     g[32 * tq:32 * tq + 32, :, :].rearrange("d (c j) t -> d j c t", j=4)[:, j]
                                     ).then_inc(g_moved, 16)

            for dst, src in LOADS:
                full = tuple(slice(None) for _ in dst.shape)
                sp.dma_start(dst[full], src).then_inc(w_loaded, 16)
            sp.dma_start(pathsel32, pathsel_in).then_inc(w_loaded, 16)

            def body(b, q, main, pre, post):
                counts = dict(transposed=NA * b + 2, half_read=UNITS * b, gates_before=4 * b, projected_0=NB * b - NB + 1,
                              xd_ready=NA * (b + 1) + 8, rows_read=64 * b, rows_stored=32 * (b + 2),
                              half_read_next=UNITS * b + DG, gates_0=4 * b + 2, projected_1=NB * b - NB + 2,
                              out_before=b, stored=16 * b)
                if not isinstance(b, int):
                    counts = {k: sp.to_reg(c) for k, c in counts.items()}
                for v in range(UNITS):
                    if v == 0 and pre:
                        reached(a_full, counts["transposed"])
                        sp.dma_start(xt[:, :, :], x_tok[b + 1]).then_inc(x_loaded, 16)
                    if v == 3 and post:
                        reshuffle(counts["gates_before"], counts["projected_0"])
                    if v == 3 and main:
                        load_bc(counts, q, 1, "half_read")
                    if v == 9 and pre:
                        reached(a_free, counts["xd_ready"])
                        reached(b_loaded[1], counts["rows_read"])
                        reached(c_loaded[1], counts["rows_read"])
                        for which in range(2):
                            sp.dma_start(bc_dram[1 - q, which], xd[DR + DS * which:DR + DS * which + DS, :]
                                         ).then_inc(bc_stored, 16)
                        reached(bc_stored, counts["rows_stored"])
                        load_bc(counts, 1 - q, 0, "half_read_next")
                    if v == 11 and main:
                        reshuffle(counts["gates_0"], counts["projected_1"])
                    if v == 13 and post:
                        reached(out_ready, counts["out_before"])
                        sp.dma_start(out_tok[b - 1], s[:, :, :]).then_inc(out_stored, 16)
                    if v == 13 and main:
                        reached(out_stored, counts["stored"])
                        sp.dma_start(s[:, :, :], x_tok[b]).then_inc(xr_loaded, 16)

            program(sp, body)
            sp.wait_ge(out_stored, 16 * BATCH)
            sp.wait_ge(bc_stored, 32 * BATCH)

        @block.tensor
        def _(pe):
            pe.wait_ge(w_loaded, LOADED)
            pe.wait_ge(tables_ready, 2)
            mm = nc.tensor.matmul

            def job_a(b, k):
                need(pe, a_free, NA * b + k)

            def job_b(b, k):
                need(pe, b_free[k % 2], NB // 2 * b + k // 2)
                return banks_b[k % 2]

            def replicate(b, q, v):
                h, dg = v // DG, v % DG
                w = UNITS * b + v
                cols = slice(h * HALF, (h + 1) * HALF)
                if v == 0:
                    pe.wait_ge(dt_ready, 2 * (b + 1))
                need(pe, decay_done, NG * w)
                mm(dt_bank[:, :], selrep[:, dg % 4, :], dtv[q][:, dg // 4, cols],
                   start=True, stop=True).then_inc(dt_rep_full, 1)
                need(pe, dbu_done, w - 1)
                mm(du_bank[v % 2][:, :], selrep[:, dg % 4, :], duv[q][:, dg // 4, cols],
                   start=True, stop=True).then_inc(du_rep_full, 1)

            def sum_states(b, q, v):
                h, dg = v // DG, v % DG
                k, col = dg // 4, (dg % 4) * P
                pe.wait_ge(cmul_done, UNITS * b + v + 1)
                if dg % 4 == 0:
                    need(pe, gate_done, 4 * b + 2 * h + k - 1)
                for n in range(NG + 1):
                    for tq in range(TQ):
                        o = y_bank[k][32 * tq:32 * tq + 32, col:col + P]
                        if n == 0:
                            t0 = h * HALF + tq * P
                            last = mm(o, seld[:, k, dg % 4, :], u[q][:, k, t0:t0 + P], start=True, stop=False)
                        else:
                            last = mm(o, ssum[:, :], st[:, v % XR, n - 1, tq * P:(tq + 1) * P],
                                      start=False, stop=n == NG)
                last.then_inc(ysum_done, 1)

            def body(b, q, main, pre, post):
                c = b + 1
                for v in range(UNITS):
                    if v >= 2 and main:
                        sum_states(b, q, v - 2)
                    if v < 2 and post:
                        sum_states(b - 1, 1 - q, v + UNITS - 2)

                    if v == 2 and main:
                        need(pe, a_free, NA * b + 2)
                        for h in range(2):
                            for k in range(2):
                                job_a(b, 12 + 2 * h + k)
                                for j in range(4):
                                    for tq in range(TQ):
                                        d0 = DI + (4 * k + j) * DW
                                        t0 = h * HALF + tq * P
                                        last = mm(bank_a[32 * tq:32 * tq + 32, j * P:(j + 1) * P],
                                                  wxz[:, d0:d0 + DW], ht[:, t0:t0 + P], start=True, stop=True)
                                last.then_inc(a_full, 1)
                    if v == 4 and pre:
                        pe.wait_ge(ln0_done, c + 1)
                        for h in range(2):
                            job_a(c, h)
                            for t in range(TQ):
                                last = nc.tensor.transpose(bank_a[:, t * P:(t + 1) * P], xt[:, TQ * h + t, :],
                                                           ident[:, :])
                            last.then_inc(a_full, 1)
                    if v in (5, 6) and pre:
                        k = v - 5
                        for h in range(2):
                            job_a(c, 2 + 2 * k + h)
                            mm(bank_a[:, :], wxz[:, k * P:(k + 1) * P], ht[:, h * HALF:(h + 1) * HALF],
                               start=True, stop=True).then_inc(a_full, 1)
                    if v == 8 and pre:
                        pe.wait_ge(u_ready, 2 * (c + 1))
                        for h in range(2):
                            job_a(c, 6 + h)
                            for k in range(BLK):
                                last = mm(bank_a[0:DR + 2 * DS, :], xpw[:, k, :],
                                          u[1 - q][:, k, h * HALF:(h + 1) * HALF], start=k == 0, stop=k == BLK - 1)
                            last.then_inc(a_full, 1)
                    if v in (9, 10) and pre:
                        k = v - 9
                        for h in range(2):
                            job_a(c, 8 + 2 * k + h)
                            mm(bank_a[:, :], dtw[:, k * P:(k + 1) * P], xd[:, h * HALF:(h + 1) * HALF],
                               start=True, stop=True).then_inc(a_full, 1)

                    o = b if v == 15 else b - 1
                    if (v == 15 and main) or (v == 3 and post):
                        h = 0 if v == 15 else 1
                        bank = job_b(o, h)
                        pe.wait_ge(g_moved, 256 * (2 * o + h + 1))
                        for tq in range(TQ):
                            for k in range(BLK):
                                last = mm(bank[:, tq * DM:(tq + 1) * DM], g_blk[:, k, tq, :], wo[:, k, :],
                                          start=k == 0, stop=k == BLK - 1)
                        last.then_inc(b_full, 1)
                    if v == 5 and post:
                        pe.wait_ge(ln1_done, b)
                        for h in range(2):
                            bank = job_b(b - 1, 2 + h)
                            for t in range(TQ):
                                last = nc.tensor.transpose(bank[:, t * P:(t + 1) * P], x1[:, TQ * h + t, :],
                                                           ident[:, :])
                            last.then_inc(b_full, 1)
                    if v in (9, 11) and post:
                        k8 = 4 + 9 * (0 if v == 9 else 1) + 8
                        bank = job_b(b - 1, k8)
                        pe.wait_ge(b_free[(k8 - 1) % 2], NB // 2 * (b - 1) + (k8 - 1) // 2 + 1)
                        for t in range(TQ):
                            for k in range(3):
                                last = mm(bank[:, t * DM:(t + 1) * DM], hid[:, k, t * P:(t + 1) * P], w2[:, k, :],
                                          start=k == 0, stop=k == 2)
                        last.then_inc(b_full, 1)
                    if v in (7, 9) and post:
                        h = 0 if v == 7 else 1
                        base = 4 + 9 * h
                        pe.wait_ge(xmix_done, b)
                        for k in range(3):
                            m = P if k < 2 else 2 * PW
                            bank = job_b(b - 1, base + k)
                            mm(bank[0:m, :], w1[:, k * P:k * P + m], xm[:, h * HALF:(h + 1) * HALF],
                               start=True, stop=True).then_inc(b_full, 1)
                        bank = job_b(b - 1, base + 3)
                        pe.wait_ge(b_free[base % 2], NB // 2 * (b - 1) + (base + 2) // 2 + 1)
                        for t in range(TQ):
                            last = mm(bank[:, t * PATHS:(t + 1) * PATHS], hid[:, 2, t * P:(t + 1) * P], wo2[:, :],
                                      start=True, stop=True)
                        last.then_inc(b_full, 1)
                    if v in (8, 10) and post:
                        h = 0 if v == 8 else 1
                        base = 4 + 9 * h
                        bank = job_b(b - 1, base + 4)
                        pe.wait_ge(oh_ready, 2 * (b - 1) + h + 1)
                        for t in range(TQ):
                            last = nc.tensor.transpose(bank[0:PATHS, t * P:(t + 1) * P], sc[2][:, t, :], ident[:, :])
                        last.then_inc(b_full, 1)
                        pe.wait_ge(oh_copied, 2 * (b - 1) + h + 1)
                        for k in range(3):
                            bank = job_b(b - 1, base + 5 + k)
                            mm(bank[:, :], pathsel[:, k, :], oh_t[:, :], start=True, stop=True).then_inc(b_full, 1)

                    if v < UNITS - 2 and main:
                        replicate(b, q, v + 2)
                    if v >= UNITS - 2 and pre:
                        replicate(c, 1 - q, v + 2 - UNITS)

            program(pe, body)

        @block.scalar
        def _(act):
            act.wait_ge(w_loaded, LOADED)
            nc.scalar.activation(a_neg[:, :], a_neg[:, :], ACT.Exp).then_inc(a_exp, 1)
            act.wait_ge(tables_ready, 2)

            def rough_rsqrt(g_, buf, var, log, rough):
                act.wait_ge(var, g_ + 1)
                nc.scalar.activation(sm[buf][5][:, :], sm[buf][4][:, :], ACT.Ln).then_inc(log, 1)
                act.wait_ge(log, g_ + 1)
                nc.scalar.activation(sm[buf][6][:, :], sm[buf][5][:, :], ACT.Exp, scale=-0.5).then_inc(rough, 1)

            def exp_and_log_tables():
                nc.scalar.preload_act_table_set("natural_log_exp_and_others")

            def decays(b, v):
                w = UNITS * b + v
                act.wait_ge(dt_rep_full, w + 1)
                need(act, scan_done, NG * (w - 1))
                for n in range(NG):
                    k = (v % DG) * NG + n
                    nc.scalar.activation(decay[:, v % 2, n, :], dt_bank[:, :], ACT.Exp,
                                         scale=a_neg[:, k:k + 1]).then_inc(decay_done, 1)

            def body(b, q, main, pre, post):
                c = b + 1
                exp_and_log_tables()
                for v in range(UNITS):
                    if v < UNITS - 1 and main:
                        decays(b, v + 1)
                    if v == UNITS - 1 and pre:
                        decays(c, 0)

                    if v == 1 and pre:
                        rough_rsqrt(c, 0, ln0_var, ln0_log, ln0_rough)
                    if v == 2 and main:
                        need(act, gate_done, 4 * b)
                        for j in range(4):
                            act.wait_ge(a_full, NA * b + 12 + j + 1)
                            nc.scalar.activation(zs[:, j // 2, 4 * (j % 2):4 * (j % 2) + 4, :],
                                                 bank_a[:, :].rearrange("p (j t) -> p j t", j=4), ACT.Silu
                                                 ).then_inc(a_free, 1)
                        exp_and_log_tables()
                    if v == 4 and pre:
                        for h in range(2):
                            act.wait_ge(a_full, NA * c + h + 1)
                            nc.scalar.activation(ht[:, h * HALF:(h + 1) * HALF], bank_a[:, :], ACT.Identity,
                                                 scale=normw[:, 0:1], bias=normb[:, 0:1]).then_inc(a_free, 1)
                    if v in (5, 6) and pre:
                        k = v - 5
                        need(act, conv_done, 2 * c + k)
                        for h in range(2):
                            act.wait_ge(a_full, NA * c + 2 + 2 * k + h + 1)
                            nc.scalar.activation(xpad[:, DC - 1 + h * HALF:DC - 1 + (h + 1) * HALF], bank_a[:, :],
                                                 ACT.Copy).then_inc(a_free, 1)
                    if v == 7 and pre:
                        for k in range(BLK):
                            act.wait_ge(conv_done, 2 * c + k + 1)
                            nc.scalar.activation(u[1 - q][:, k, :], u[1 - q][:, k, :], ACT.Silu).then_inc(u_ready, 1)
                    if v == 8 and pre:
                        need(act, bc_stored, 32 * (b + 1))
                        for h in range(2):
                            act.wait_ge(a_full, NA * c + 6 + h + 1)
                            nc.scalar.activation(xd[:, h * HALF:(h + 1) * HALF], bank_a[0:DR + 2 * DS, :], ACT.Copy
                                                 ).then_inc(a_free, 1)
                    if v in (9, 10) and pre:
                        k = v - 9
                        for h in range(2):
                            cols = slice(h * HALF, (h + 1) * HALF)
                            act.wait_ge(a_full, NA * c + 8 + 2 * k + h + 1)
                            nc.scalar.activation(duv[1 - q][:, k, cols], bank_a[:, :], ACT.Abs, bias=dtb[:, k:k + 1]
                                                 ).then_inc(sp_abs, 1)
                            nc.scalar.activation(dtv[1 - q][:, k, cols], bank_a[:, :], ACT.Relu,
                                                 bias=dtb[:, k:k + 1]).then_inc(a_free, 1)
                        y = duv[1 - q][:, k, :]
                        act.wait_ge(sp_abs, 4 * c + 2 * k + 2)
                        nc.scalar.activation(y, y, ACT.Exp, scale=-1.0).then_inc(sp_exp, 1)
                        nc.scalar.preload_act_table_set("natural_log")
                        act.wait_ge(sp_exp, 2 * c + k + 1)
                        need(act, sp_big, 2 * c + k)
                        nc.scalar.activation(sp_ln[:, :], y, ACT.Ln, bias=1.0).then_inc(sp_log, 1)
                        need(act, sp_small, 2 * c + k)
                        nc.scalar.activation(sp_t[:, :], y, ACT.Identity, bias=1.0).then_inc(sp_round, 1)
                        exp_and_log_tables()

                    if v == 4 and post:
                        rough_rsqrt(b - 1, 1, ln_var[1], ln_log[1], ln_rough[1])
                    if v == 5 and post:
                        for h in range(2):
                            act.wait_ge(b_full, NB * (b - 1) + 2 + h + 1)
                            nc.scalar.activation(x1t[:, 1 + h * HALF:1 + (h + 1) * HALF], banks_b[h][:, :], ACT.Copy
                                                 ).then_inc(b_free[h], 1)
                    if v in (7, 9) and post:
                        h = 0 if v == 7 else 1
                        base = 4 + 9 * h
                        for k in range(3):
                            act.wait_ge(b_full, NB * (b - 1) + base + k + 1)
                            bank, free = banks_b[(base + k) % 2], b_free[(base + k) % 2]
                            if k < 2:
                                nc.scalar.activation(hid[:, k, :], bank[:, :], ACT.Identity, bias=b1[:, k:k + 1]
                                                     ).then_inc(free, 1)
                            else:
                                nc.scalar.activation(hid[0:PW, k, :], bank[0:PW, :], ACT.Identity,
                                                     bias=b1[0:PW, k:k + 1])
                                nc.scalar.activation(hid[PW:2 * PW, k, :], bank[PW:2 * PW, :], ACT.Tanh,
                                                     bias=b1[PW:2 * PW, k:k + 1]).then_inc(free, 1)
                        exp_and_log_tables()
                    if v == 7 and pre and not post:
                        exp_and_log_tables()
                    if v in (8, 10) and post:
                        h = 0 if v == 8 else 1
                        k = 4 + 9 * h + 4
                        act.wait_ge(b_full, NB * (b - 1) + k + 1)
                        nc.scalar.activation(oh_t[:, :], banks_b[k % 2][0:PATHS, :], ACT.Copy).then_inc(oh_copied, 1)
                        nc.scalar.activation(hid[PW:PW + PATHS, 2, :], banks_b[k % 2][0:PATHS, :], ACT.Copy
                                             ).then_inc(b_free[k % 2], 1)
                    if v == 11 and post:
                        rough_rsqrt(b - 1, 1, ln_var[2], ln_log[2], ln_rough[2])
                    if v == 12 and post:
                        rough_rsqrt(b - 1, 1, ln_var[3], ln_log[3], ln_rough[3])

            program(act, body)

        @block.gpsimd
        def _(pool):
            def body(b, q, main, pre, post):
                c = b + 1
                for v in range(UNITS):
                    if main:
                        h, dg, w = v // DG, v % DG, UNITS * b + v
                        pool.wait_ge(scan_done, NG * w + NG)
                        if h == 0:
                            pool.wait_ge(h_saved, DG * b + dg + 1)
                        if dg == 0:
                            pool.wait_ge(c_loaded[h], 64 * (b + 1))
                        nc.gpsimd.tensor_tensor(st[:, v % XR, :, :], st[:, v % XR, :, :], c_rep[h][:, :, :], ALU.mult
                                                ).then_inc(cmul_done, 1)
                    if v in (9, 10) and pre:
                        k = v - 9
                        dtk = dtv[1 - q][:, k, :]
                        pool.wait_ge(a_free, NA * c + 10 + 2 * k)
                        pool.wait_ge(sp_log, 2 * c + k + 1)
                        nc.gpsimd.tensor_tensor(dtk, dtk, sp_ln[:, :], ALU.add).then_inc(sp_big, 1)
                    if v in (10, 11) and pre:
                        k = v - 10
                        pool.wait_ge(sp_sum, 2 * c + k + 1)
                        nc.gpsimd.tensor_tensor(duv[1 - q][:, k, :], dtv[1 - q][:, k, :], u[1 - q][:, k, :], ALU.mult
                                                ).then_inc(dt_ready, 1)
                    if v == 11 and post:
                        pool.wait_ge(b_free[1], NB // 2 * b)
                        nc.gpsimd.tensor_tensor(x1[:, :, :], x1[:, :, :],
                                                beta[:, :].unsqueeze(1).broadcast_to([P, TILES, DM]), ALU.add
                                                ).then_inc(x1b_ready, 1)

            pool.wait_ge(w_loaded, LOADED)
            program(pool, body)

        @block.vector
        def _(dve):
            tt, ts, stt = nc.vector.tensor_tensor, nc.vector.tensor_scalar, nc.vector.scalar_tensor_tensor
            before = Steps(dve, pre_step, PRE_STEPS)
            after = Steps(dve, post_step, POST_STEPS)

            nc.vector.memset(xpad[:, 0:DC - 1], 0.0)
            nc.vector.memset(x1t[:, 0:1], 0.0)
            nc.vector.memset(x1t[:, SEQ + 1:SEQ + 2], 0.0)
            nc.vector.memset(hid[:, 2, :], 0.0).then_inc(tables_ready, 1)
            dve.wait_ge(w_loaded, LOADED)
            dve.wait_ge(a_exp, 1)
            ts(a_neg[:, :], a_neg[:, :], -1.0, None, ALU.mult)
            nc.vector.tensor_copy(pathsel[:, :, :], pathsel32.rearrange("p (k n) -> p k n", k=3))
            for k in range(BLK):
                last = ts(seld[:, k, :, :], sel32[:, :, :], dpar[:, k:k + 1], None, ALU.mult)
            last.then_inc(tables_ready, 1)
            dve.wait_ge(tables_ready, 2)

            def statistics(steps, buf, src):
                mean, diff, var2, _, veps = sm[buf][0:5]
                for t in range(TILES):
                    last = nc.vector.bn_stats(bn[buf][:, t, :], src[:, t, :])
                steps.did(last)
                steps.wait()
                tt(mean[:, :], bn[buf][:, :, 1], bn[buf][:, :, 4], ALU.add)
                tt(diff[:, :], bn[buf][:, :, 1], bn[buf][:, :, 4], ALU.subtract)
                steps.did(tt(var2[:, :], bn[buf][:, :, 2], bn[buf][:, :, 5], ALU.add))
                steps.wait()
                ts(mean[:, :], mean[:, :], 0.5, None, ALU.mult)
                ts(var2[:, :], var2[:, :], 1.0 / DM, EPS, ALU.mult, ALU.add)
                steps.did(stt(diff[:, :], diff[:, :], 0.25, diff[:, :], ALU.mult, ALU.mult))
                steps.wait()
                return tt(veps[:, :], diff[:, :], var2[:, :], ALU.add)

            def refine(steps, buf):
                _, q_, _, _, veps, _, r0, r = sm[buf]
                steps.did(tt(q_[:, :], r0[:, :], r0[:, :], ALU.mult))
                steps.wait()
                steps.did(tt(q_[:, :], q_[:, :], veps[:, :], ALU.mult))
                steps.wait()
                steps.did(ts(q_[:, :], q_[:, :], -0.5, 1.5, ALU.mult, ALU.add))
                steps.wait()
                steps.did(tt(r[:, :], r0[:, :], q_[:, :], ALU.mult))
                steps.wait()

            def normalise(buf, dst, src):
                mean, r = sm[buf][0], sm[buf][7]
                for t in range(TILES):
                    last = ts(dst[:, t, :], src[:, t, :], mean[:, t:t + 1], r[:, t:t + 1], ALU.subtract, ALU.mult)
                return last

            def body(b, q, main, pre, post):
                c = b + 1
                for v in range(UNITS):
                    if main:
                        h, dg, w, r = v // DG, v % DG, UNITS * b + v, v % XR
                        dve.wait_ge(du_rep_full, w + 1)
                        need(dve, ysum_done, w - XR + 1)
                        if dg == 0:
                            dve.wait_ge(b_loaded[h], 64 * (b + 1))
                        tt(st[:, r, :, :], du_bank[v % 2][:, :].unsqueeze(1).broadcast_to([P, NG, HALF]),
                           b_rep[h][:, :, :], ALU.mult).then_inc(dbu_done, 1)
                    if v in (9, 11) and post:
                        hh = 0 if v == 9 else 1
                        for k in range(3):
                            m = P if k < 2 else PW
                            j = 4 + 9 * hh + 5 + k
                            dve.wait_ge(b_full, NB * (b - 1) + j + 1)
                            tt(hid[0:m, k, :], hid[0:m, k, :], banks_b[j % 2][0:m, :], ALU.mult
                               ).then_inc(b_free[j % 2], 1)
                    if main:
                        dve.wait_ge(dbu_done, w + 1)
                        if h == 1:
                            dve.wait_ge(h_saved, DG * b + dg + 1)
                        for n in range(NG):
                            dve.wait_ge(decay_done, NG * w + n + 1)
                            nc.vector.tensor_tensor_scan(st[:, r, n, :], decay[:, v % 2, n, :], st[:, r, n, :],
                                                         h_last[:, dg, n:n + 1] if h else 0.0,
                                                         ALU.mult, ALU.add).then_inc(scan_done, 1)
                        if h == 0:
                            dve.wait_ge(scan_done, NG * w + NG)
                            nc.vector.tensor_copy(h_last[:, dg, :], st[:, r, :, HALF - 1]).then_inc(h_saved, 1)

                    gates = {6: (b, 0, 0), 10: (b, 0, 1), 14: (b, 1, 0), 2: (b - 1, 1, 1)}
                    if v in gates and (post if v == 2 else main):
                        o, gh, k = gates[v]
                        dve.wait_ge(ysum_done, UNITS * o + DG * gh + 4 * k + 4)
                        dve.wait_ge(a_free, NA * o + 16)
                        need(dve, g_moved, 256 * (2 * o + gh))
                        tt(g[:, 4 * k:4 * k + 4, :], y_bank[k][:, :].rearrange("p (j t) -> p j t", j=4),
                           zs[:, gh, 4 * k:4 * k + 4, :], ALU.mult).then_inc(gate_done, 1)

                    if v == 0 and pre:
                        before.begin(c)
                        dve.wait_ge(x_loaded, 16 * (c + 1))
                        statistics(before, 0, xt).then_inc(ln0_var, 1)
                    if v == 2 and pre:
                        dve.wait_ge(ln0_var, c + 1)
                        dve.wait_ge(ln0_rough, c + 1)
                        refine(before, 0)
                        normalise(0, xt, xt).then_inc(ln0_done, 1)
                    if v in (6, 7) and pre:
                        k = v - 6
                        dve.wait_ge(a_free, NA * c + 4 + 2 * k)
                        dst = u[1 - q][:, k, :]
                        before.did(ts(dst, xpad[:, 0:SEQ], convw[:, k, 0:1], convb[:, k:k + 1], ALU.mult, ALU.add))
                        for i in (1, 2):
                            before.wait()
                            before.did(stt(dst, xpad[:, i:i + SEQ], convw[:, k, i:i + 1], dst, ALU.mult, ALU.add))
                        before.wait()
                        stt(dst, xpad[:, 3:3 + SEQ], convw[:, k, 3:4], dst, ALU.mult, ALU.add).then_inc(conv_done, 1)
                    if v in (10, 11) and pre:
                        k = v - 10
                        y, dtk, n = duv[1 - q][:, k, :], dtv[1 - q][:, k, :], 2 * c + k + 1
                        dve.wait_ge(sp_round, n)
                        stt(y, sp_t[:, :], 1.0, y, ALU.subtract, ALU.subtract).then_inc(sp_small, 1)
                        dve.wait_ge(sp_small, n)
                        dve.wait_ge(sp_big, n)
                        tt(dtk, dtk, y, ALU.subtract).then_inc(sp_sum, 1)
                    if v == 11 and pre:
                        before.end()

                    o = b if v == 15 else b - 1
                    if (v == 15 and main) or (v == 4 and post):
                        h = 0 if v == 15 else 1
                        if h == 0:
                            dve.wait_ge(xr_loaded, 16 * (o + 1))
                        dve.wait_ge(b_full, NB * o + h + 1)
                        sh = s[:, TQ * h:TQ * h + TQ, :]
                        stt(sh, sh, 2.0, banks_b[h][:, :].rearrange("p (t m) -> p t m", t=TQ), ALU.mult, ALU.add
                            ).then_inc(b_free[h], 1)
                    if v == 4 and post:
                        after.begin(b - 1)
                        dve.wait_ge(b_free[1], NB // 2 * (b - 1) + 1)
                        statistics(after, 1, s).then_inc(ln_var[1], 1)
                    if v == 5 and post:
                        dve.wait_ge(ln_rough[1], b)
                        refine(after, 1)
                        normalise(1, x1, s).then_inc(ln1_done, 1)
                    if v == 6 and post:
                        for h in range(2):
                            dve.wait_ge(b_free[h], NB // 2 * (b - 1) + 2)
                        after.did(ts(xm[:, :], x1t[:, 0:SEQ], mix[:, 0:1], None, ALU.mult))
                        after.wait()
                        after.did(stt(xm[:, :], x1t[:, 1:1 + SEQ], mix[:, 1:2], xm[:, :], ALU.mult, ALU.add))
                        after.wait()
                        stt(xm[:, :], x1t[:, 2:2 + SEQ], mix[:, 2:3], xm[:, :], ALU.mult, ALU.add).then_inc(xmix_done, 1)
                    if v in (9, 11) and post:
                        hh = 0 if v == 9 else 1
                        k = 4 + 9 * hh + 8
                        dve.wait_ge(b_full, NB * (b - 1) + k + 1)
                        tt(s[:, TQ * hh:TQ * hh + TQ, :], x1[:, TQ * hh:TQ * hh + TQ, :],
                           banks_b[k % 2][:, :].rearrange("p (t m) -> p t m", t=TQ), ALU.add
                           ).then_inc(b_free[k % 2], 1)
                    if v in (8, 10) and post:
                        hh = 0 if v == 8 else 1
                        base = 4 + 9 * hh
                        k = base + 3
                        wide = [P, TQ, PATHS]
                        dve.wait_ge(b_full, NB * (b - 1) + k + 1)
                        tt(sc[0][:, :, :], banks_b[k % 2][:, 0:TQ * PATHS].rearrange("p (t n) -> p t n", t=TQ),
                           bo2[:, :].unsqueeze(1).broadcast_to(wide), ALU.add).then_inc(b_free[k % 2], 1)
                        dve.wait_ge(b_free[k % 2], NB // 2 * (b - 1) + k // 2 + 1)
                        after.did(nc.vector.tensor_reduce(scm[0][:, :], sc[0][:, :, :], AX.X, ALU.max))
                        after.wait()
                        after.did(tt(sc[1][:, :, :], sc[0][:, :, :], scm[0][:, :].unsqueeze(2).broadcast_to(wide),
                                     ALU.is_equal))
                        after.wait()
                        after.did(tt(sc[1][:, :, :], sc[1][:, :, :], desc[:, :].unsqueeze(1).broadcast_to(wide),
                                     ALU.mult))
                        after.wait()
                        after.did(nc.vector.tensor_reduce(scm[1][:, :], sc[1][:, :, :], AX.X, ALU.max))
                        after.wait()
                        tt(sc[2][:, :, :], sc[1][:, :, :], scm[1][:, :].unsqueeze(2).broadcast_to(wide),
                           ALU.is_equal).then_inc(oh_ready, 1)
                    if v == 11 and post:
                        for i in range(2):
                            dve.wait_ge(b_free[i], NB // 2 * b)
                        statistics(after, 1, s).then_inc(ln_var[2], 1)
                    if v == 12 and post:
                        dve.wait_ge(ln_rough[2], b)
                        refine(after, 1)
                        after.did(normalise(1, s, s))
                        after.wait()
                        after.did(tt(s[:, :, :], s[:, :, :], gamma[:, :].unsqueeze(1).broadcast_to([P, TILES, DM]),
                                     ALU.mult))
                        after.wait()
                        dve.wait_ge(x1b_ready, b)
                        after.did(tt(s[:, :, :], s[:, :, :], x1[:, :, :], ALU.add))
                        after.wait()
                        statistics(after, 1, s).then_inc(ln_var[3], 1)
                    if v == 13 and post:
                        dve.wait_ge(ln_rough[3], b)
                        refine(after, 1)
                        normalise(1, s, s).then_inc(out_ready, 1)
                        after.end()

            program(dve, body)


def kernel(**inputs):
    import numpy as _np
    import concourse.bacc as _bacc
    from concourse import mybir as _mybir
    from concourse.bass_utils import run_bass_kernel_spmd as _run

    A = {k.replace("L0_", ""): _np.ascontiguousarray(v) for k, v in inputs.items()}
    F = _np.float32

    def blocks(v):
        return v.reshape((2, 128) + v.shape[1:]).swapaxes(0, 1)

    w1 = _np.zeros((128, 320), F)
    w1[:, 0:288] = A["ffn_W1"].transpose(1, 0, 2).reshape(128, 288)
    w1[:, 288:320] = A["ffn_Wo1"]
    b1 = _np.zeros((384,), F)
    b1[0:288] = A["ffn_b1"].reshape(288)
    b1[288:320] = A["ffn_bo1"]
    w2 = _np.zeros((384, 128), F)
    w2[0:288] = A["ffn_W2"].reshape(288, 128)
    w2[288:297] = A["ffn_b2"]
    wo2 = _np.zeros((128, 9), F)
    wo2[32:64] = A["ffn_Wo2"]
    dtw = _np.zeros((96, 256), F)
    dtw[0:64] = A["attn_dt_proj_w"].T
    selrep = _np.zeros((128, 4, 4, 32), F)
    sel32 = _np.zeros((128, 4, 32), F)
    ssum = _np.zeros((4, 32, 32), F)
    pathsel = _np.zeros((9, 384), F)
    for j in range(4):
        for d in range(32):
            selrep[32 * j + d, j, :, d] = 1
            sel32[32 * j + d, j, d] = 1
            ssum[j, d, d] = 1
    for p in range(9):
        pathsel[p, 32 * p:32 * p + 32] = 1
    arrays = [
        ("x", A["attn_hidden_states"]),
        ("wxz", A["attn_in_proj_w"].T),
        ("convw", blocks(A["attn_conv_w"][:, 0, :])),
        ("convb", blocks(A["attn_conv_b"])),
        ("normw", A["attn_norm_w"].reshape(128, 1)),
        ("normb", A["attn_norm_b"].reshape(128, 1)),
        ("xpw", blocks(A["attn_x_proj_w"].T)),
        ("dtw", dtw),
        ("dtb", blocks(A["attn_dt_proj_b"])),
        ("alog", A["attn_A_log"].reshape(8, 32, 4, 4).transpose(3, 1, 0, 2).reshape(128, 32)),
        ("dpar", blocks(A["attn_D"])),
        ("wo", blocks(A["attn_out_proj_w"].T)),
        ("mix", A["ffn_mix_kernel"].T),
        ("w1", w1),
        ("b1", b1.reshape(3, 128).T),
        ("w2", w2.reshape(3, 128, 128).transpose(1, 0, 2)),
        ("wo2", wo2),
        ("bo2", _np.broadcast_to(A["ffn_bo2"], (128, 9))),
        ("gamma", _np.broadcast_to(A["ffn_gamma"], (128, 128))),
        ("beta", _np.broadcast_to(A["ffn_beta"], (128, 128))),
        ("ident", _np.eye(128, dtype=F)),
        ("selrep", selrep.reshape(128, 4, 128)),
        ("sel32", sel32),
        ("ssum", ssum.reshape(128, 32)),
        ("pathsel", pathsel),
        ("desc", _np.broadcast_to(_np.arange(9, 0, -1).astype(F), (128, 9))),
    ]
    nc = _bacc.Bacc("TRN2", target_bir_lowering=False, num_devices=1)
    feeds, args = {}, []
    for name, a in arrays:
        a = _np.ascontiguousarray(a)
        feeds[f"in_{name}"] = a
        args.append(nc.dram_tensor(f"in_{name}", a.shape, _mybir.dt.float32, kind="ExternalInput").ap())
    args.append(nc.dram_tensor("out_y", (8, 1024, 128), _mybir.dt.float32, kind="ExternalOutput").ap())
    build(nc, *args)
    r = _run(nc, [feeds], core_ids=[0])
    return r.results[0]["out_y"]
```

```python
import numpy as np
import concourse.bass as bass
from concourse import mybir
from contextlib import ExitStack

f32 = mybir.dt.float32
bf16 = mybir.dt.bfloat16
ALU = mybir.AluOpType
ACT = mybir.ActivationFunctionType
AX = mybir.AxisListType

BATCH, SEQ, DM = 8, 1024, 128
DI, DS, DC, DR = 256, 16, 4, 64
PATHS, PW = 9, 32
P = 128
TILES = SEQ // P
HALF = SEQ // 2
TQ = HALF // P
BLK = DI // P
DG, DW = DI // 32, 32
NG = DS // 4
UNITS = 2 * DG
XR = 4
EPS = 1e-5
NA = 16
PRE_STEPS, POST_STEPS = 10, 26


JOBS_B = [("project0", 0), ("project1", 1), ("x1t0", 0), ("x1t1", 1), ("router", 0), ("H00", 1), ("H01", 1),
          ("scores", 1), ("H02", 0), ("H10", 0), ("choice", 1), ("H11", 0), ("M00", 1), ("H12", 0), ("M02", 0),
          ("M01", 1), ("M10", 0), ("M11", 1), ("M12", 0), ("Y0", 1), ("Y1", 0)]
NB = len(JOBS_B)
BANK_B = dict(JOBS_B)
NUMBER_B = {name: i for i, (name, _) in enumerate(JOBS_B)}
IN_BANK_B = {name: sum(bank == b for _, b in JOBS_B[:i]) for i, (name, bank) in enumerate(JOBS_B)}
OF_BANK_B = [sum(bank == i for _, bank in JOBS_B) for i in range(2)]


COLUMNS = dict(convw=BLK * DC, convb=BLK, normw=1, normb=1, dtb=BLK, alog=DG * NG, dpar=BLK, mix=3, b1=4,
               wo2=2 * PATHS, bo2=PATHS, desc=PATHS)
COLUMN_START = {name: sum(list(COLUMNS.values())[:i]) for i, name in enumerate(COLUMNS)}




def need(eng, sem, count):
    if not isinstance(count, int) or count > 0:
        eng.wait_ge(sem, count)


def job_a(c, kind, k):
    at = dict(transpose=0, x=2, z=6 if k < 2 else 12, x_dbl=8, dt=10)[kind] + k
    if isinstance(c, int) and c == 0:
        return at if at < 6 else at - 2
    if isinstance(c, int) and c == BATCH:
        at = k
    return NA * c - 4 + at


def full_b(o, name):
    return NB * o + NUMBER_B[name] + 1


def free_b(o, name):
    return OF_BANK_B[BANK_B[name]] * o + IN_BANK_B[name] + 1


class Steps:

    def __init__(self, eng, sem, total):
        self.eng, self.sem, self.total, self.k, self.g = eng, sem, total, 0, 0

    def begin(self, g):
        self.g, self.k = g, 0

    def did(self, ins):
        self.k += 1
        ins.then_inc(self.sem, 1)

    def wait(self):
        need(self.eng, self.sem, self.g * self.total + self.k)

    def end(self):
        assert self.k == self.total, (self.k, self.total)


def build(nc, x_in, columns_in, ident_in, wxz_in, xpw_in, dtw_in, selrep_in, ssum_in, wo_in, w1_in, w2_in,
          gamma_in, beta_in, pathsel_in, out):
    x_tok = x_in.rearrange("b (n p) m -> b p n m", p=P)
    out_tok = out.rearrange("b (n p) m -> b p n m", p=P)
    g_dram = nc.dram_tensor("gated", [P, DG, P], f32, kind="Internal").ap()
    bc_dram = nc.dram_tensor("bc_rows", [2, 2, DS, SEQ], f32, kind="Internal").ap()

    with ExitStack() as ctx:
        def sb(name, shape, dt=f32):
            return ctx.enter_context(nc.sbuf_tensor(name, shape, dt))

        def ps(name, shape, dt=f32):
            return ctx.enter_context(nc.psum_tensor(name, shape, dt))

        def sem(name):
            return ctx.enter_context(nc.semaphore(name))

        columns = sb("columns", [P, sum(COLUMNS.values())])

        def column(name, rows=None):
            start = COLUMN_START[name]
            cols = columns[:, start:start + COLUMNS[name]]
            return cols if rows is None else cols.rearrange("p (a b) -> p a b", a=rows)

        convw = column("convw", BLK)
        convb = column("convb")
        normw = column("normw")
        normb = column("normb")
        dtb = column("dtb")
        a_neg = column("alog")
        dpar = column("dpar")
        mix = column("mix")
        b1 = column("b1")
        wo2 = column("wo2", 2)
        bo2 = column("bo2")
        desc = column("desc")
        wxz = sb("wxz", [P, 2 * DI])
        xpw = sb("xpw", [P, BLK, DR + 2 * DS])
        dtw = sb("dtw", [DR + 2 * DS, DI])
        wo = sb("wo", [P, BLK, DM])
        w1 = sb("w1", [P, PATHS * PW + PW])
        w2 = sb("w2", [P, 3, DM])
        gamma = sb("gamma", [P, DM])
        beta = sb("beta", [P, DM])
        ident = sb("ident", [P, P])
        selrep = sb("selrep", [P, 4, P])
        seld = sb("seld", [P, BLK, 4, DW])
        ssum = sb("ssum", [P, DW])
        pathsel = sb("pathsel", [P, 3, P], bf16)

        xt = sb("xt", [P, TILES, DM])
        ht = [sb(f"ht{q}", [P, SEQ]) for q in range(2)]
        xpad = sb("xpad", [P, BLK, DC - 1 + SEQ])
        sp_ln = xpad[:, 0, DC - 1:]
        sp_t = xpad[:, 1, DC - 1:]
        xd = sb("xd", [DR + 2 * DS, SEQ])
        dtv = [sb(f"dtv{q}", [P, BLK, SEQ]) for q in range(2)]
        duv = [sb(f"duv{q}", [P, BLK, SEQ]) for q in range(2)]
        u = [sb(f"u{q}", [P, BLK, SEQ]) for q in range(2)]
        zs = sb("zs", [P, 2, DG, P])
        b_rep = [sb(f"b_rep{h}", [P, NG, HALF]) for h in range(2)]
        c_rep = [sb(f"c_rep{h}", [P, NG, HALF]) for h in range(2)]
        decay = sb("decay", [P, 2, NG, 1 + HALF])
        st = sb("st", [P, XR, NG, 1 + HALF])
        h_last = sb("h_last", [P, DG, NG])
        g = sb("g", [P, DG, P])
        g_blk = sb("g_blk", [P, BLK, TQ, P])
        s = sb("s", [P, TILES, DM])
        x1 = sb("x1", [P, TILES, DM])
        x1t = sb("x1t", [P, SEQ + 2])
        xm = sb("xm", [P, SEQ])
        hid = [sb("hid0", [P, 2, HALF]), xt[:, :, :].rearrange("p t m -> p (t m)").rearrange("p (k n) -> p k n", k=2)]
        hid8 = [sb(f"hid8_{h}", [P, HALF]) for h in range(2)]
        pathsel32 = xm[:, 0:3 * P]
        oh_t = hid8[1][:, :].bitcast(bf16)[:, 0:HALF]
        bn = [sb(f"bn{k}", [P, TILES, 6]) for k in range(2)]
        sm = [[sb(f"sm{k}_{i}", [P, TILES]) for i in range(8)] for k in range(2)]
        sc = [sb(f"sc{i}", [P, TILES, PATHS]) for i in range(3)]
        scm = [sb(f"scm{i}", [P, TILES]) for i in range(2)]

        dt_bank = ps("dt_bank", [P, HALF])
        du_bank = [ps(f"du_bank{i}", [P, HALF]) for i in range(2)]
        y_bank = [ps(f"y_bank{i}", [P, 4 * P]) for i in range(2)]
        bank_a = ps("bank_a", [P, 512])
        banks_b = [ps(f"bank_b{i}", [P, 512]) for i in range(2)]

        first_loaded = sem("first_loaded")
        w_loaded = sem("w_loaded")
        tables_ready = sem("tables_ready")
        a_exp = sem("a_exp")
        x_loaded = sem("x_loaded")
        ln0_var = sem("ln0_var")
        ln0_log = sem("ln0_log")
        ln0_rough = sem("ln0_rough")
        ln0_scale = sem("ln0_scale")
        ln0_done = sem("ln0_done")
        a_full = sem("a_full")
        a_free = sem("a_free")
        tap0_done = sem("tap0_done")
        conv_done = sem("conv_done")
        u_ready = sem("u_ready")
        sp_abs = sem("sp_abs")
        sp_exp = sem("sp_exp")
        sp_log = sem("sp_log")
        sp_round = sem("sp_round")
        sp_small = sem("sp_small")
        sp_big = sem("sp_big")
        sp_sum = sem("sp_sum")
        dt_ready = sem("dt_ready")
        bc_stored = sem("bc_stored")
        b_loaded = [sem(f"b_loaded{h}") for h in range(2)]
        c_loaded = [sem(f"c_loaded{h}") for h in range(2)]
        pre_step = sem("pre_step")
        post_step = sem("post_step")
        dt_rep_full = sem("dt_rep_full")
        du_rep_full = sem("du_rep_full")
        decay_done = sem("decay_done")
        dbu_done = sem("dbu_done")
        scan_done = sem("scan_done")
        h_saved = sem("h_saved")
        cmul_done = sem("cmul_done")
        ysum_done = sem("ysum_done")
        gate_done = sem("gate_done")
        g_saved = sem("g_saved")
        g_moved = sem("g_moved")
        xr_loaded = sem("xr_loaded")
        b_full = sem("b_full")
        b_free = [sem(f"b_free{i}") for i in range(2)]
        ln_var = [None] + [sem(f"ln{k}_var") for k in (1, 2, 3)]
        ln_log = [None] + [sem(f"ln{k}_log") for k in (1, 2, 3)]
        ln_rough = [None] + [sem(f"ln{k}_rough") for k in (1, 2, 3)]
        ln_scale = [None] + [sem(f"ln{k}_scale") for k in (1, 2, 3)]
        ln1_done = sem("ln1_done")
        ln2_done = sem("ln2_done")
        xmix_done = sem("xmix_done")
        oh_ready = sem("oh_ready")
        oh_copied = sem("oh_copied")
        x1b_ready = sem("x1b_ready")
        out_ready = sem("out_ready")
        s_free = sem("s_free")

        FIRST_LOADS = [(columns, columns_in), (ident, ident_in), (wxz, wxz_in)]
        LOADS = [(xpw, xpw_in), (dtw, dtw_in), (selrep, selrep_in), (ssum, ssum_in), (pathsel32, pathsel_in),
                 (wo, wo_in), (w1, w1_in), (w2, w2_in), (gamma, gamma_in), (beta, beta_in)]
        FIRST_LOADED, LOADED = 16 * len(FIRST_LOADS), 16 * len(LOADS)

        block = ctx.enter_context(nc.Block())

        def program(eng, body):
            body(-1, 1, False, True, False)
            body(0, 0, True, True, False)
            with eng.Fori(0, (BATCH - 2) // 2) as pair:
                body(2 * pair + 1, 1, True, True, True)
                body(2 * pair + 2, 0, True, True, True)
            body(BATCH - 1, (BATCH - 1) % 2, True, False, True)
            body(BATCH, BATCH % 2, False, False, True)

        @block.sync
        def _(sp):
            def reached(sem, count):
                need(sp, sem, count)

            def load_bc(counts, q, h, loaded_by):
                for which, rep, sem_, used in ((0, b_rep, b_loaded, dbu_done), (1, c_rep, c_loaded, cmul_done)):
                    reached(used, counts[loaded_by])
                    for n in range(4):
                        rows = bc_dram[q, which].rearrange("(g n) t -> n g t", n=4)[n, :, h * HALF:(h + 1) * HALF]
                        sp.dma_start(rep[h][32 * n:32 * n + 32, :, :],
                                     rows.unsqueeze(0).broadcast_to([32, NG, HALF])).then_inc(sem_[h], 16)

            def reshuffle(gates, projected, saved):
                reached(gate_done, gates)
                reached(b_full, projected)
                sp.dma_start(g_dram, g[:, :, :]).then_inc(g_saved, 16)
                reached(g_saved, saved)
                for j in range(4):
                    sp.dma_start(g_blk[32 * j:32 * j + 32, :, :, :],
                                 g_dram.rearrange("(t d) (k j) n -> j d k t n", d=32, j=4)[j]).then_inc(g_moved, 16)

            def load(dst, src, sem):
                full = tuple(slice(None) for _ in dst.shape)
                sp.dma_start(dst[full], src).then_inc(sem, 16)

            load(xt, x_tok[0], x_loaded)
            for dst, src in FIRST_LOADS:
                load(dst, src, first_loaded)
            for dst, src in LOADS:
                load(dst, src, w_loaded)

            def body(b, q, main, pre, post):
                counts = dict(half_read=UNITS * b, half_read_next=UNITS * b + DG, gates_before=4 * b,
                              gates_0=4 * b + 2, saved_0=16 * (2 * b + 1), saved_1=32 * b,
                              projected_0=full_b(b - 1, "project0"), projected_1=full_b(b - 1, "project1"),
                              xd_ready=job_a(b + 1, "x_dbl", 1) + 1, rows_read=64 * b, rows_stored=32 * (b + 2),
                              out_before=b, stored=16 * b)
                if not isinstance(b, int):
                    counts = {k: sp.to_reg(c) for k, c in counts.items()}
                for v in range(UNITS):
                    if v == 0 and pre and main:
                        if post:
                            reached(b_full, counts["projected_0"])
                        else:
                            reached(a_full, 2)
                        sp.dma_start(xt[:, :, :], x_tok[b + 1]).then_inc(x_loaded, 16)
                    if v == 0 and post:
                        reached(s_free, counts["stored"])
                        sp.dma_start(s[:, :, :], x_tok[b - 1]).then_inc(xr_loaded, 16)
                    if v == 1 and post:
                        reshuffle(counts["gates_before"], counts["projected_0"], counts["saved_1"])
                    if v == 3 and main:
                        load_bc(counts, q, 1, "half_read")
                    if v == 9 and pre:
                        reached(a_free, counts["xd_ready"])
                        reached(b_loaded[1], counts["rows_read"])
                        reached(c_loaded[1], counts["rows_read"])
                        for which in range(2):
                            sp.dma_start(bc_dram[1 - q, which], xd[DR + DS * which:DR + DS * which + DS, :]
                                         ).then_inc(bc_stored, 16)
                        reached(bc_stored, counts["rows_stored"])
                        load_bc(counts, 1 - q, 0, "half_read_next")
                    if v == 11 and main:
                        reshuffle(counts["gates_0"], counts["projected_1"], counts["saved_0"])
                    if v == 15 and post:
                        reached(out_ready, counts["out_before"])
                        sp.dma_start(out_tok[b - 1], s[:, :, :]).then_inc(s_free, 16)

            program(sp, body)
            sp.wait_ge(s_free, 16 * (BATCH + 1))
            sp.wait_ge(bc_stored, 32 * BATCH)
            sp.wait_ge(g_saved, 32 * BATCH)

        @block.tensor
        def _(pe):
            pe.wait_ge(first_loaded, FIRST_LOADED)
            mm = nc.tensor.matmul

            def bank_a_free(c, kind, k):
                need(pe, a_free, job_a(c, kind, k))

            def job_b(o, name):
                i = BANK_B[name]
                need(pe, b_free[i], free_b(o, name) - 1)
                return banks_b[i]

            def replicate(b, q, v):
                h, dg = v // DG, v % DG
                w = UNITS * b + v
                cols = slice(h * HALF, (h + 1) * HALF)
                if h == 0 and dg % 4 == 0:
                    pe.wait_ge(dt_ready, 2 * b + dg // 4 + 1)
                need(pe, decay_done, NG * w)
                mm(dt_bank[:, :], selrep[:, dg % 4, :], dtv[q][:, dg // 4, cols],
                   start=True, stop=True).then_inc(dt_rep_full, 1)
                need(pe, dbu_done, w - 1)
                mm(du_bank[v % 2][:, :], selrep[:, dg % 4, :], duv[q][:, dg // 4, cols],
                   start=True, stop=True).then_inc(du_rep_full, 1)

            def sum_states(b, q, v):
                h, dg = v // DG, v % DG
                k, col = dg // 4, (dg % 4) * P
                pe.wait_ge(cmul_done, UNITS * b + v + 1)
                if dg % 4 == 0:
                    need(pe, gate_done, 4 * b + 2 * h + k - 1)
                for n in range(NG + 1):
                    for tq in range(TQ):
                        o = y_bank[k][32 * tq:32 * tq + 32, col:col + P]
                        if n == 0:
                            t0 = h * HALF + tq * P
                            last = mm(o, seld[:, k, dg % 4, :], u[q][:, k, t0:t0 + P], start=True, stop=False)
                        else:
                            last = mm(o, ssum[:, :], st[:, v % XR, n - 1, 1 + tq * P:1 + (tq + 1) * P],
                                      start=False, stop=n == NG)
                last.then_inc(ysum_done, 1)

            def transpose_tokens(c, q, h):
                bank_a_free(c, "transpose", h)
                for t in range(TQ):
                    last = nc.tensor.transpose(bank_a[:, t * P:(t + 1) * P], xt[:, TQ * h + t, :], ident[:, :])
                last.then_inc(a_full, 1)

            def project_x(c, q, k, h):
                bank_a_free(c, "x", 2 * k + h)
                mm(bank_a[:, :], wxz[:, k * P:(k + 1) * P], ht[q][:, h * HALF:(h + 1) * HALF],
                   start=True, stop=True).then_inc(a_full, 1)

            def project_z(b, q, h, k):
                bank_a_free(b + 1, "z", 2 * h + k)
                for j in range(4):
                    for tq in range(TQ):
                        d0 = DI + (4 * k + j) * DW
                        t0 = h * HALF + tq * P
                        last = mm(bank_a[32 * tq:32 * tq + 32, j * P:(j + 1) * P],
                                  wxz[:, d0:d0 + DW], ht[q][:, t0:t0 + P], start=True, stop=True)
                last.then_inc(a_full, 1)

            def project_dbl(c, q, h):
                if h == 0:
                    if isinstance(c, int) and c == 0:
                        pe.wait_ge(w_loaded, LOADED)
                        pe.wait_ge(tables_ready, 3)
                    pe.wait_ge(u_ready, 2 * (c + 1))
                bank_a_free(c, "x_dbl", h)
                for k in range(BLK):
                    last = mm(bank_a[0:DR + 2 * DS, :], xpw[:, k, :],
                              u[q][:, k, h * HALF:(h + 1) * HALF], start=k == 0, stop=k == BLK - 1)
                last.then_inc(a_full, 1)

            def project_dt(c, k, h):
                bank_a_free(c, "dt", 2 * k + h)
                mm(bank_a[:, :], dtw[:, k * P:(k + 1) * P], xd[:, h * HALF:(h + 1) * HALF],
                   start=True, stop=True).then_inc(a_full, 1)

            def project_out(o, h):
                if h == 0:
                    bank = job_b(o, "project0")
                else:
                    bank = banks_b[BANK_B["project1"]]
                pe.wait_ge(g_moved, 64 * (2 * o + h + 1))
                for tq in range(TQ):
                    for k in range(BLK):
                        last = mm(bank[:, tq * DM:(tq + 1) * DM], g_blk[:, k, tq, :], wo[:, k, :],
                                  start=k == 0, stop=k == BLK - 1)
                last.then_inc(b_full, 1)

            def transpose_x1(o, h):
                bank = job_b(o, f"x1t{h}")
                pe.wait_ge(ln1_done, o + 1)
                for t in range(TQ):
                    last = nc.tensor.transpose(bank[:, t * P:(t + 1) * P], x1[:, TQ * h + t, :], ident[:, :])
                last.then_inc(b_full, 1)

            def router(o):
                bank = job_b(o, "router")
                pe.wait_ge(xmix_done, o + 1)
                for h in range(2):
                    r0 = 2 * PW + h * PW
                    last = mm(bank[r0:r0 + PW, :], w1[:, PATHS * PW:PATHS * PW + PW],
                              xm[:, h * HALF:(h + 1) * HALF], start=True, stop=True)
                last.then_inc(b_full, 1)

            def scores(o):
                bank = job_b(o, "scores")
                pe.wait_ge(b_free[BANK_B["router"]], free_b(o, "router"))
                for t in range(TILES):
                    last = mm(bank[:, t * PATHS:(t + 1) * PATHS],
                              hid8[0][2 * PW:4 * PW, (t % TQ) * P:(t % TQ + 1) * P], wo2[2 * PW:4 * PW, t // TQ, :],
                              start=True, stop=True)
                last.then_inc(b_full, 1)

            def choice(o):
                bank = job_b(o, "choice")
                pe.wait_ge(oh_ready, o + 1)
                for t in range(TILES):
                    r0 = PW * (2 + t // TQ)
                    last = mm(bank[r0:r0 + PATHS, (t % TQ) * P:(t % TQ + 1) * P], sc[2][:, t, :], ident[:, :],
                              start=True, stop=True)
                last.then_inc(b_full, 1)

            def hidden(o, h, k):
                m = P if k < 2 else PW
                bank = job_b(o, f"H{h}{k}")
                mm(bank[0:m, :], w1[:, k * P:k * P + m], xm[:, h * HALF:(h + 1) * HALF],
                   start=True, stop=True).then_inc(b_full, 1)

            def mask(o, h, k):
                bank = job_b(o, f"M{h}{k}")
                pe.wait_ge(oh_copied, o + 1)
                rows = slice(PW * (2 + h), PW * (2 + h) + PATHS)
                mm(bank[:, :], pathsel[rows, k, :], oh_t[rows, :],
                   start=True, stop=True).then_inc(b_full, 1)

            def second(o, h):
                bank = job_b(o, f"Y{h}")
                masked = f"M{h}{2 - h}"
                pe.wait_ge(b_free[BANK_B[masked]], free_b(o, masked))
                for t in range(TQ):
                    tok = slice(t * P, (t + 1) * P)
                    for k in range(2):
                        mm(bank[:, t * DM:(t + 1) * DM], hid[h][:, k, tok], w2[:, k, :], start=k == 0, stop=False)
                    last = mm(bank[:, t * DM:(t + 1) * DM], hid8[h][0:PW + PATHS, tok], w2[0:PW + PATHS, 2, :],
                              start=False, stop=True)
                last.then_inc(b_full, 1)

            def early(b, q, v, main, pre, post):
                c, o = b + 1, b - 1
                if v == 4 and pre:
                    transpose_tokens(c, 1 - q, 1)
                if v == 5 and pre:
                    project_x(c, 1 - q, 0, 1)
                if v == 6 and pre:
                    project_x(c, 1 - q, 1, 1)
                if v == 7 and post:
                    hidden(o, 0, 1)
                if v == 7 and main:
                    project_z(b, q, 0, 0)
                if v == 8 and post:
                    hidden(o, 1, 0)
                if v == 9 and post:
                    mask(o, 0, 0)
                    hidden(o, 1, 2)
                if v == 9 and pre:
                    project_dbl(c, 1 - q, 0)
                if v == 11 and post:
                    mask(o, 1, 0)
                    mask(o, 1, 1)
                if v == 11 and pre:
                    project_dt(c, 0, 1)
                if v == 12 and pre:
                    project_dt(c, 1, 1)
                if v == 14 and main:
                    project_z(b, q, 1, 0)
                if v == 15 and main:
                    project_out(b, 0)

            def late(b, q, v, main, pre, post):
                c, o = b + 1, b - 1
                if v == 3 and post:
                    project_out(o, 1)
                if v == 3 and pre:
                    pe.wait_ge(ln0_done, c + 1)
                    transpose_tokens(c, 1 - q, 0)
                if v == 4 and pre:
                    project_x(c, 1 - q, 0, 0)
                if v == 5 and post:
                    transpose_x1(o, 0)
                    transpose_x1(o, 1)
                if v == 5 and pre:
                    project_x(c, 1 - q, 1, 0)
                if v == 6 and post:
                    router(o)
                    hidden(o, 0, 0)
                if v == 7 and main:
                    project_z(b, q, 0, 1)
                if v == 7 and post:
                    scores(o)
                    hidden(o, 0, 2)
                if v == 8 and post:
                    choice(o)
                    hidden(o, 1, 1)
                if v == 9 and post:
                    mask(o, 0, 2)
                    mask(o, 0, 1)
                if v == 9 and pre:
                    project_dbl(c, 1 - q, 1)
                if v == 10 and pre:
                    project_dt(c, 0, 0)
                if v == 11 and post:
                    mask(o, 1, 2)
                    second(o, 0)
                if v == 11 and pre:
                    project_dt(c, 1, 0)
                if v == 11 and post:
                    second(o, 1)
                if v == 14 and main:
                    project_z(b, q, 1, 1)

            def body(b, q, main, pre, post):
                c = b + 1
                for v in range(UNITS):
                    if v >= 2 and main:
                        sum_states(b, q, v - 2)
                    if v < 2 and post:
                        sum_states(b - 1, 1 - q, v + UNITS - 2)
                    early(b, q, v, main, pre, post)
                    if v < UNITS - 2 and main:
                        replicate(b, q, v + 2)
                    if v >= UNITS - 2 and pre:
                        replicate(c, 1 - q, v + 2 - UNITS)
                    late(b, q, v, main, pre, post)

            program(pe, body)

        @block.scalar
        def _(act):
            act.wait_ge(first_loaded, FIRST_LOADED)
            nc.scalar.activation(a_neg[:, :], a_neg[:, :], ACT.Exp).then_inc(a_exp, 1)

            def rough_rsqrt(g_, buf, var, log, rough):
                act.wait_ge(var, g_ + 1)
                nc.scalar.activation(sm[buf][5][:, :], sm[buf][4][:, :], ACT.Ln).then_inc(log, 1)
                act.wait_ge(log, g_ + 1)
                nc.scalar.activation(sm[buf][6][:, :], sm[buf][5][:, :], ACT.Exp, scale=-0.5).then_inc(rough, 1)

            def normalise(g_, buf, scale, dst, src):
                act.wait_ge(scale, g_ + 1)
                for t in range(TILES):
                    last = nc.scalar.activation(dst[:, t, :], src[:, t, :], ACT.Identity, scale=sm[buf][7][:, t:t + 1],
                                                bias=sm[buf][3][:, t:t + 1])
                return last

            def exp_and_log_tables():
                nc.scalar.preload_act_table_set("natural_log_exp_and_others")

            def decays(b, v):
                if isinstance(b, int) and b == 0 and v == 0:
                    act.wait_ge(tables_ready, 2)
                w = UNITS * b + v
                act.wait_ge(dt_rep_full, w + 1)
                need(act, scan_done, w - 1)
                for n in range(NG):
                    k = (v % DG) * NG + n
                    nc.scalar.activation(decay[:, v % 2, n, 1:], dt_bank[:, :], ACT.Exp,
                                         scale=a_neg[:, k:k + 1]).then_inc(decay_done, 1)

            def copy_transposed(c, q, h):
                act.wait_ge(a_full, job_a(c, "transpose", h) + 1)
                nc.scalar.activation(ht[q][:, h * HALF:(h + 1) * HALF], bank_a[:, :], ACT.Identity,
                                     scale=normw[:, 0:1], bias=normb[:, 0:1]).then_inc(a_free, 1)

            def copy_x(c, q, k, h):
                if k == 0 and h == 0:
                    need(act, sp_sum, 2 * c)
                act.wait_ge(a_full, job_a(c, "x", 2 * k + h) + 1)
                nc.scalar.activation(xpad[:, k, DC - 1 + h * HALF:DC - 1 + (h + 1) * HALF], bank_a[:, :],
                                     ACT.Copy).then_inc(a_free, 1)
                if h == 1:
                    act.wait_ge(a_free, job_a(c, "x", 2 * k + 1) + 1)
                    if k == 0:
                        need(act, ysum_done, UNITS * (c - 1))
                    nc.scalar.activation(u[q][:, k, :], xpad[:, k, 0:SEQ], ACT.Identity, scale=convw[:, k, 0:1],
                                         bias=convb[:, k:k + 1]).then_inc(tap0_done, 1)

            def silu_z(b, h, k):
                if h == 0 and k == 0:
                    need(act, gate_done, 4 * b)
                act.wait_ge(a_full, job_a(b + 1, "z", 2 * h + k) + 1)
                nc.scalar.activation(zs[:, h, 4 * k:4 * k + 4, :],
                                     bank_a[:, :].rearrange("p (j t) -> p j t", j=4), ACT.Silu).then_inc(a_free, 1)

            def silu_u(c, q, k):
                act.wait_ge(conv_done, 2 * c + k + 1)
                nc.scalar.activation(u[q][:, k, :], u[q][:, k, :], ACT.Silu).then_inc(u_ready, 1)

            def copy_dbl(c, h):
                if h == 0:
                    need(act, bc_stored, 32 * c)
                act.wait_ge(a_full, job_a(c, "x_dbl", h) + 1)
                nc.scalar.activation(xd[:, h * HALF:(h + 1) * HALF], bank_a[0:DR + 2 * DS, :], ACT.Copy
                                     ).then_inc(a_free, 1)

            def softplus_parts(c, q, k, h):
                cols = slice(h * HALF, (h + 1) * HALF)
                act.wait_ge(a_full, job_a(c, "dt", 2 * k + h) + 1)
                nc.scalar.activation(duv[q][:, k, cols], bank_a[:, :], ACT.Abs, bias=dtb[:, k:k + 1]
                                     ).then_inc(sp_abs, 1)
                nc.scalar.activation(dtv[q][:, k, cols], bank_a[:, :], ACT.Relu, bias=dtb[:, k:k + 1]
                                     ).then_inc(a_free, 1)

            def softplus_log(c, q, k):
                y = duv[q][:, k, :]
                act.wait_ge(sp_abs, 4 * c + 2 * k + 2)
                nc.scalar.activation(y, y, ACT.Exp, scale=-1.0).then_inc(sp_exp, 1)
                nc.scalar.preload_act_table_set("natural_log")
                act.wait_ge(sp_exp, 2 * c + k + 1)
                need(act, sp_big, 2 * c + k)
                nc.scalar.activation(sp_ln, y, ACT.Ln, bias=1.0).then_inc(sp_log, 1)
                need(act, sp_small, 2 * c + k)
                nc.scalar.activation(sp_t, y, ACT.Identity, bias=1.0).then_inc(sp_round, 1)
                exp_and_log_tables()

            def copy_x1(o, h):
                act.wait_ge(b_full, full_b(o, f"x1t{h}"))
                nc.scalar.activation(x1t[:, 1 + h * HALF:1 + (h + 1) * HALF], banks_b[BANK_B[f"x1t{h}"]][:, :],
                                     ACT.Copy).then_inc(b_free[BANK_B[f"x1t{h}"]], 1)

            def tanh_router(o):
                act.wait_ge(b_full, full_b(o, "router"))
                i = BANK_B["router"]
                nc.scalar.activation(hid8[0][2 * PW:4 * PW, :], banks_b[i][2 * PW:4 * PW, :], ACT.Tanh,
                                     bias=b1[2 * PW:4 * PW, 3:4]).then_inc(b_free[i], 1)

            def add_bias(o, h, k):
                i = BANK_B[f"H{h}{k}"]
                act.wait_ge(b_full, full_b(o, f"H{h}{k}"))
                m = P if k < 2 else PW
                dst = hid[h][:, k, :] if k < 2 else hid8[h][0:PW, :]
                nc.scalar.activation(dst, banks_b[i][0:m, :], ACT.Identity, bias=b1[0:m, k:k + 1]
                                     ).then_inc(b_free[i], 1)

            def copy_choice(o):
                i = BANK_B["choice"]
                act.wait_ge(b_full, full_b(o, "choice"))
                for h in range(2):
                    rows = slice(PW * (2 + h), PW * (2 + h) + PATHS)
                    last = nc.scalar.activation(oh_t[rows, :], banks_b[i][rows, :], ACT.Copy)
                last.then_inc(oh_copied, 1)
                for h in range(2):
                    rows = slice(PW * (2 + h), PW * (2 + h) + PATHS)
                    last = nc.scalar.activation(hid8[h][PW:PW + PATHS, :], banks_b[i][rows, :], ACT.Copy)
                last.then_inc(b_free[i], 1)

            def first(b, q, v, main, pre, post):
                c, o = b + 1, b - 1
                if v == 4 and pre:
                    copy_transposed(c, 1 - q, 0)
                if v == 5 and pre:
                    copy_x(c, 1 - q, 0, 0)
                if v == 6 and post:
                    copy_x1(o, 0)
                    copy_x1(o, 1)
                if v == 6 and pre:
                    copy_x(c, 1 - q, 1, 0)
                if v == 7 and post:
                    add_bias(o, 0, 0)
                if v == 8 and post:
                    add_bias(o, 0, 2)
                if v == 9 and post:
                    copy_choice(o)
                    add_bias(o, 1, 1)
                if v == 11 and pre:
                    softplus_parts(c, 1 - q, 0, 0)
                if v == 12 and pre:
                    softplus_parts(c, 1 - q, 1, 0)
                if v == 13 and post:
                    rough_rsqrt(o, 1, ln_var[2], ln_log[2], ln_rough[2])

            def second(b, q, v, main, pre, post):
                c, o = b + 1, b - 1
                if v == 2 and pre:
                    rough_rsqrt(c, 0, ln0_var, ln0_log, ln0_rough)
                if v == 3 and pre:
                    act.wait_ge(x_loaded, 16 * (c + 1))
                    normalise(c, 0, ln0_scale, xt, xt).then_inc(ln0_done, 1)
                if v == 4 and pre:
                    copy_transposed(c, 1 - q, 1)
                if v == 4 and post:
                    rough_rsqrt(o, 1, ln_var[1], ln_log[1], ln_rough[1])
                if v == 5 and post:
                    normalise(o, 1, ln_scale[1], x1, s).then_inc(ln1_done, 1)
                if v == 5 and pre:
                    copy_x(c, 1 - q, 0, 1)
                if v == 6 and pre:
                    copy_x(c, 1 - q, 1, 1)
                if v == 7 and post:
                    add_bias(o, 0, 1)
                    tanh_router(o)
                if v == 7 and main:
                    silu_z(b, 0, 0)
                    silu_z(b, 0, 1)
                if v == 8 and post:
                    add_bias(o, 1, 0)
                if v == 8 and pre:
                    silu_u(c, 1 - q, 0)
                    silu_u(c, 1 - q, 1)
                if v == 9 and post:
                    add_bias(o, 1, 2)
                if v == 9 and pre:
                    copy_dbl(c, 0)
                if v == 10 and pre:
                    copy_dbl(c, 1)
                if v == 11 and pre:
                    softplus_parts(c, 1 - q, 0, 1)
                    softplus_log(c, 1 - q, 0)
                if v == 12 and pre:
                    softplus_parts(c, 1 - q, 1, 1)
                if v == 13 and post:
                    normalise(o, 1, ln_scale[2], s, s).then_inc(ln2_done, 1)
                if v == 13 and pre and not main:
                    decays(c, 0)
                if v == 13 and pre:
                    softplus_log(c, 1 - q, 1)
                if v == 14 and post:
                    rough_rsqrt(o, 1, ln_var[3], ln_log[3], ln_rough[3])
                if v == 14 and main:
                    silu_z(b, 1, 0)
                    silu_z(b, 1, 1)
                if v == 7 or (v == 8 and pre) or (v == 14 and main):
                    exp_and_log_tables()
                if v == 15 and post:
                    normalise(o, 1, ln_scale[3], s, s).then_inc(out_ready, 1)

            exp_and_log_tables()

            def body(b, q, main, pre, post):
                for v in range(UNITS):
                    first(b, q, v, main, pre, post)
                    if v < UNITS - 1 and main:
                        decays(b, v + 1)
                    if v == UNITS - 1 and pre and main:
                        decays(b + 1, 0)
                    second(b, q, v, main, pre, post)

            program(act, body)

        @block.gpsimd
        def _(pool):
            def body(b, q, main, pre, post):
                c = b + 1
                for v in range(UNITS):
                    if main:
                        h, dg, w = v // DG, v % DG, UNITS * b + v
                        pool.wait_ge(scan_done, w + 1)
                        if h == 0:
                            pool.wait_ge(h_saved, DG * b + dg + 1)
                        if dg == 0:
                            pool.wait_ge(c_loaded[h], 64 * (b + 1))
                        nc.gpsimd.tensor_tensor(st[:, v % XR, :, 1:], st[:, v % XR, :, 1:], c_rep[h][:, :, :], ALU.mult
                                                ).then_inc(cmul_done, 1)
                    if v in (11, 14) and pre and not main:
                        k = (v - 11) // 3
                        dtk = dtv[1 - q][:, k, :]
                        pool.wait_ge(a_free, job_a(c, "dt", 2 * k + 1) + 1)
                        pool.wait_ge(sp_log, k + 1)
                        nc.gpsimd.tensor_tensor(dtk, dtk, sp_ln, ALU.add).then_inc(sp_big, 1)
                    if v in (11, 14) and pre and main:
                        k = (v - 11) // 3
                        y, dtk = duv[1 - q][:, k, :], dtv[1 - q][:, k, :]
                        pool.wait_ge(a_free, job_a(c, "dt", 2 * k + 1) + 1)
                        pool.wait_ge(sp_log, 2 * c + k + 1)
                        nc.gpsimd.tensor_tensor(dtk, dtk, sp_ln, ALU.add).then_inc(sp_big, 1)
                        pool.wait_ge(sp_big, 2 * c + k + 1)
                        pool.wait_ge(sp_small, 2 * c + k + 1)
                        nc.gpsimd.tensor_tensor(dtk, dtk, y, ALU.subtract).then_inc(sp_sum, 1)
                    if v in (12, 15) and pre and main:
                        k = (v - 12) // 3
                        pool.wait_ge(sp_sum, 2 * c + k + 1)
                        nc.gpsimd.tensor_tensor(duv[1 - q][:, k, :], dtv[1 - q][:, k, :], u[1 - q][:, k, :], ALU.mult
                                                ).then_inc(dt_ready, 1)
                    if v == 12 and post:
                        pool.wait_ge(b_free[BANK_B["Y0"]], free_b(b - 1, "Y0"))
                        pool.wait_ge(b_free[BANK_B["Y1"]], free_b(b - 1, "Y1"))
                        nc.gpsimd.tensor_tensor(x1[:, :, :], x1[:, :, :],
                                                beta[:, :].unsqueeze(1).broadcast_to([P, TILES, DM]), ALU.add
                                                ).then_inc(x1b_ready, 1)

            pool.wait_ge(w_loaded, LOADED)
            program(pool, body)

        @block.vector
        def _(dve):
            tt, ts, stt = nc.vector.tensor_tensor, nc.vector.tensor_scalar, nc.vector.scalar_tensor_tensor
            before = Steps(dve, pre_step, PRE_STEPS)
            after = Steps(dve, post_step, POST_STEPS)

            nc.vector.memset(xpad[:, :, 0:DC - 1], 0.0)
            nc.vector.memset(x1t[:, 0:1], 0.0).then_inc(s_free, 16)
            nc.vector.memset(decay[:, :, :, 0], 0.0)
            nc.vector.memset(x1t[:, SEQ + 1:SEQ + 2], 0.0).then_inc(tables_ready, 1)
            dve.wait_ge(first_loaded, FIRST_LOADED)
            dve.wait_ge(a_exp, 1)
            ts(a_neg[:, :], a_neg[:, :], -1.0, None, ALU.mult)
            for k in range(BLK):
                last = ts(seld[:, k, :, :], ident[:, :].rearrange("p (j d) -> p j d", j=4), dpar[:, k:k + 1], None, ALU.mult)
            last.then_inc(tables_ready, 1)
            dve.wait_ge(tables_ready, 2)

            def statistics(steps, buf, src):
                mean, diff, var2, _, veps = sm[buf][0:5]
                for t in range(TILES):
                    last = nc.vector.bn_stats(bn[buf][:, t, :], src[:, t, :])
                steps.did(last)
                steps.wait()
                tt(mean[:, :], bn[buf][:, :, 1], bn[buf][:, :, 4], ALU.add)
                tt(diff[:, :], bn[buf][:, :, 1], bn[buf][:, :, 4], ALU.subtract)
                steps.did(tt(var2[:, :], bn[buf][:, :, 2], bn[buf][:, :, 5], ALU.add))
                steps.wait()
                ts(var2[:, :], var2[:, :], 1.0 / DM, EPS, ALU.mult, ALU.add)
                steps.did(stt(diff[:, :], diff[:, :], 0.25, diff[:, :], ALU.mult, ALU.mult))
                steps.wait()
                return tt(veps[:, :], diff[:, :], var2[:, :], ALU.add)

            def refine(steps, buf):
                mean, q_, _, shift, veps, _, r0, r = sm[buf]
                steps.did(stt(q_[:, :], veps[:, :], -0.5, r0[:, :], ALU.mult, ALU.mult))
                steps.wait()
                steps.did(tt(q_[:, :], q_[:, :], r0[:, :], ALU.mult))
                steps.wait()
                steps.did(stt(r[:, :], q_[:, :], 1.5, r0[:, :], ALU.add, ALU.mult))
                steps.wait()
                return stt(shift[:, :], mean[:, :], -0.5, r[:, :], ALU.mult, ALU.mult)

            def product_with_b(b, v):
                h, dg, w, r = v // DG, v % DG, UNITS * b + v, v % XR
                dve.wait_ge(du_rep_full, w + 1)
                need(dve, ysum_done, w - XR + 1)
                if dg == 0:
                    dve.wait_ge(b_loaded[h], 64 * (b + 1))
                if h == 0:
                    nc.vector.memset(st[:, r, :, 0], 0.0)
                else:
                    dve.wait_ge(h_saved, DG * b + dg + 1)
                    nc.vector.tensor_copy(st[:, r, :, 0], h_last[:, dg, :])
                tt(st[:, r, :, 1:], du_bank[v % 2][:, :].unsqueeze(1).broadcast_to([P, NG, HALF]),
                   b_rep[h][:, :, :], ALU.mult).then_inc(dbu_done, 1)

            def scan(b, v):
                h, dg, w, r = v // DG, v % DG, UNITS * b + v, v % XR
                dve.wait_ge(dbu_done, w + 1)
                dve.wait_ge(decay_done, NG * (w + 1))
                states = st[:, r, :, :].rearrange("p n t -> p (n t)")
                nc.vector.tensor_tensor_scan(states, decay[:, v % 2, :, :].rearrange("p n t -> p (n t)"), states, 0.0,
                                             ALU.mult, ALU.add).then_inc(scan_done, 1)
                if h == 0:
                    dve.wait_ge(scan_done, w + 1)
                    nc.vector.tensor_copy(h_last[:, dg, :], st[:, r, :, HALF]).then_inc(h_saved, 1)

            def gate(o, gh, k):
                dve.wait_ge(ysum_done, UNITS * o + DG * gh + 4 * k + 4)
                dve.wait_ge(a_free, job_a(o + 1, "z", 2 * gh + k) + 1)
                need(dve, g_saved, 16 * (2 * o + gh))
                tt(g[:, 4 * k:4 * k + 4, :], y_bank[k][:, :].rearrange("p (j t) -> p j t", j=4),
                   zs[:, gh, 4 * k:4 * k + 4, :], ALU.mult).then_inc(gate_done, 1)

            def add_residual(o, h):
                i = BANK_B[f"project{h}"]
                dve.wait_ge(b_full, full_b(o, f"project{h}"))
                sh = s[:, TQ * h:TQ * h + TQ, :]
                stt(sh, sh, 2.0, banks_b[i][:, :].rearrange("p (t m) -> p t m", t=TQ), ALU.mult, ALU.add
                    ).then_inc(b_free[i], 1)

            def mix_tokens(o):
                for h in range(2):
                    dve.wait_ge(b_free[BANK_B[f"x1t{h}"]], free_b(o, f"x1t{h}"))
                after.did(ts(xm[:, :], x1t[:, 0:SEQ], mix[:, 0:1], None, ALU.mult))
                after.wait()
                after.did(stt(xm[:, :], x1t[:, 1:1 + SEQ], mix[:, 1:2], xm[:, :], ALU.mult, ALU.add))
                after.wait()
                stt(xm[:, :], x1t[:, 2:2 + SEQ], mix[:, 2:3], xm[:, :], ALU.mult, ALU.add).then_inc(xmix_done, 1)

            def choose(o):
                i, wide = BANK_B["scores"], [P, TILES, PATHS]
                dve.wait_ge(b_full, full_b(o, "scores"))
                tt(sc[0][:, :, :], banks_b[i][:, 0:TILES * PATHS].rearrange("p (t n) -> p t n", t=TILES),
                   bo2[:, :].unsqueeze(1).broadcast_to(wide), ALU.add).then_inc(b_free[i], 1)
                dve.wait_ge(b_free[i], free_b(o, "scores"))
                after.did(nc.vector.tensor_reduce(scm[0][:, :], sc[0][:, :, :], AX.X, ALU.max))
                after.wait()
                after.did(tt(sc[1][:, :, :], sc[0][:, :, :], scm[0][:, :].unsqueeze(2).broadcast_to(wide),
                             ALU.is_equal))
                after.wait()
                after.did(tt(sc[1][:, :, :], sc[1][:, :, :], desc[:, :].unsqueeze(1).broadcast_to(wide), ALU.mult))
                after.wait()
                after.did(nc.vector.tensor_reduce(scm[1][:, :], sc[1][:, :, :], AX.X, ALU.max))
                after.wait()
                tt(sc[2][:, :, :], sc[1][:, :, :], scm[1][:, :].unsqueeze(2).broadcast_to(wide), ALU.is_equal
                   ).then_inc(oh_ready, 1)

            def keep_chosen(o, h, k):
                i = BANK_B[f"M{h}{k}"]
                dst = hid[h][:, k, :] if k < 2 else hid8[h][0:PW, :]
                m = P if k < 2 else PW
                dve.wait_ge(b_free[BANK_B[f"H{h}{k}"]], free_b(o, f"H{h}{k}"))
                dve.wait_ge(b_full, full_b(o, f"M{h}{k}"))
                tt(dst, dst, banks_b[i][0:m, :], ALU.mult).then_inc(b_free[i], 1)

            def add_ffn(o, h):
                i = BANK_B[f"Y{h}"]
                dve.wait_ge(b_full, full_b(o, f"Y{h}"))
                tt(s[:, TQ * h:TQ * h + TQ, :], x1[:, TQ * h:TQ * h + TQ, :],
                   banks_b[i][:, :].rearrange("p (t m) -> p t m", t=TQ), ALU.add).then_inc(b_free[i], 1)

            def convolve(c, q, k):
                dve.wait_ge(tap0_done, 2 * c + k + 1)
                dst = u[q][:, k, :]
                for i in (1, 2):
                    before.did(stt(dst, xpad[:, k, i:i + SEQ], convw[:, k, i:i + 1], dst, ALU.mult, ALU.add))
                    before.wait()
                stt(dst, xpad[:, k, 3:3 + SEQ], convw[:, k, 3:4], dst, ALU.mult, ALU.add).then_inc(conv_done, 1)

            def correct_log(c, q, k):
                y = duv[q][:, k, :]
                dve.wait_ge(sp_round, 2 * c + k + 1)
                stt(y, sp_t, 1.0, y, ALU.subtract, ALU.subtract).then_inc(sp_small, 1)
                if isinstance(c, int) and c == 0:
                    dtk = dtv[q][:, k, :]
                    dve.wait_ge(sp_small, k + 1)
                    dve.wait_ge(sp_big, k + 1)
                    tt(dtk, dtk, y, ALU.subtract).then_inc(sp_sum, 1)
                    dve.wait_ge(sp_sum, k + 1)
                    tt(y, dtk, u[q][:, k, :], ALU.mult).then_inc(dt_ready, 1)

            def between(b, q, v, main, pre, post):
                c, o = b + 1, b - 1
                if v == 2 and post:
                    gate(o, 1, 1)
                if v in (8, 10, 15) and main:
                    gate(b, (8, 10, 15).index(v) // 2, (8, 10, 15).index(v) % 2)
                if v == 4 and post:
                    after.begin(o)
                    dve.wait_ge(xr_loaded, 16 * b)
                    add_residual(o, 0)
                    add_residual(o, 1)
                    dve.wait_ge(b_free[0], free_b(o, "project0"))
                    dve.wait_ge(b_free[1], free_b(o, "project1"))
                    statistics(after, 1, s).then_inc(ln_var[1], 1)
                if v == 6 and post:
                    mix_tokens(o)
                if v == 8 and post:
                    choose(o)
                if v == 11 and post:
                    keep_chosen(o, 1, 0)
                    keep_chosen(o, 1, 1)
                if v == 12 and post:
                    add_ffn(o, 0)
                if v == 12 and pre:
                    correct_log(c, 1 - q, 0)
                if v == 15 and pre and main:
                    correct_log(c, 1 - q, 1)
                if v == 13 and post:
                    dve.wait_ge(ln_rough[2], o + 1)
                    refine(after, 1).then_inc(ln_scale[2], 1)
                if v == 14 and post:
                    dve.wait_ge(ln2_done, o + 1)
                    after.did(tt(s[:, :, :], s[:, :, :], gamma[:, :].unsqueeze(1).broadcast_to([P, TILES, DM]),
                                 ALU.mult))
                    after.wait()
                    dve.wait_ge(x1b_ready, o + 1)
                    after.did(tt(s[:, :, :], s[:, :, :], x1[:, :, :], ALU.add))
                    after.wait()
                    statistics(after, 1, s).then_inc(ln_var[3], 1)

            def behind(b, q, v, main, pre, post):
                c, o = b + 1, b - 1
                if v == 0 and main and not post:
                    correct_log(b, q, 1)
                if v == 1 and pre:
                    before.begin(c)
                    dve.wait_ge(x_loaded, 16 * (c + 1))
                    statistics(before, 0, xt).then_inc(ln0_var, 1)
                if v == 3 and not main and pre:
                    dve.wait_ge(w_loaded, LOADED)
                    nc.vector.tensor_copy(pathsel[:, :, :], pathsel32.rearrange("p (k n) -> p k n", k=3)
                                          ).then_inc(tables_ready, 1)
                if v == 2 and pre:
                    dve.wait_ge(ln0_var, c + 1)
                    dve.wait_ge(ln0_rough, c + 1)
                    refine(before, 0).then_inc(ln0_scale, 1)
                if v == 4 and post:
                    dve.wait_ge(ln_rough[1], o + 1)
                    refine(after, 1).then_inc(ln_scale[1], 1)
                if v == 6 and pre:
                    convolve(c, 1 - q, 0)
                if v == 7 and pre:
                    convolve(c, 1 - q, 1)
                    before.end()
                if v == 9 and post:
                    keep_chosen(o, 0, 0)
                if v == 10 and post:
                    keep_chosen(o, 0, 1)
                    keep_chosen(o, 0, 2)
                if v == 11 and post:
                    keep_chosen(o, 1, 2)
                if v == 12 and post:
                    add_ffn(o, 1)
                    for h in range(2):
                        dve.wait_ge(b_free[BANK_B[f"Y{h}"]], free_b(o, f"Y{h}"))
                    statistics(after, 1, s).then_inc(ln_var[2], 1)
                if v == 14 and post:
                    dve.wait_ge(ln_rough[3], o + 1)
                    refine(after, 1).then_inc(ln_scale[3], 1)
                    after.end()

            def body(b, q, main, pre, post):
                for v in range(UNITS):
                    if main:
                        product_with_b(b, v)
                    between(b, q, v, main, pre, post)
                    if main:
                        scan(b, v)
                    behind(b, q, v, main, pre, post)

            program(dve, body)


def kernel(**inputs):
    import numpy as _np
    import concourse.bacc as _bacc
    from concourse import mybir as _mybir
    from concourse.bass_utils import run_bass_kernel_spmd as _run

    A = {k.replace("L0_", ""): _np.ascontiguousarray(v) for k, v in inputs.items()}
    F = _np.float32

    def blocks(v):
        return v.reshape((2, 128) + v.shape[1:]).swapaxes(0, 1)

    w1 = _np.zeros((128, 320), F)
    w1[:, 0:288] = A["ffn_W1"].transpose(1, 0, 2).reshape(128, 288)
    w1[:, 288:320] = A["ffn_Wo1"]
    b1 = _np.zeros((512,), F)
    b1[0:288] = A["ffn_b1"].reshape(288)
    b1[448:480] = b1[480:512] = A["ffn_bo1"]
    w2 = _np.zeros((384, 128), F)
    w2[0:288] = A["ffn_W2"].reshape(288, 128)
    w2[288:297] = A["ffn_b2"]
    wo2 = _np.zeros((128, 2, 9), F)
    wo2[64:96, 0] = wo2[96:128, 1] = A["ffn_Wo2"]
    dtw = _np.zeros((96, 256), F)
    dtw[0:64] = A["attn_dt_proj_w"].T
    selrep = _np.zeros((128, 4, 4, 32), F)
    ssum = _np.zeros((4, 32, 32), F)
    pathsel = _np.zeros((128, 384), F)
    for j in range(4):
        for d in range(32):
            selrep[32 * j + d, j, :, d] = 1
            ssum[j, d, d] = 1
    for p in range(9):
        pathsel[64 + p, 32 * p:32 * p + 32] = pathsel[96 + p, 32 * p:32 * p + 32] = 1
    columns = _np.concatenate([v.reshape(128, -1) for v in (
        blocks(A["attn_conv_w"][:, 0, :]), blocks(A["attn_conv_b"]), A["attn_norm_w"], A["attn_norm_b"],
        blocks(A["attn_dt_proj_b"]), A["attn_A_log"].reshape(8, 32, 4, 4).transpose(3, 1, 0, 2),
        blocks(A["attn_D"]), A["ffn_mix_kernel"].T, b1.reshape(4, 128).T, wo2,
        _np.broadcast_to(A["ffn_bo2"], (128, 9)), _np.broadcast_to(_np.arange(9, 0, -1).astype(F), (128, 9)))],
        axis=1)
    arrays = [
        ("x", A["attn_hidden_states"]),
        ("columns", columns),
        ("ident", _np.eye(128, dtype=F)),
        ("wxz", A["attn_in_proj_w"].T),
        ("xpw", blocks(A["attn_x_proj_w"].T)),
        ("dtw", dtw),
        ("selrep", selrep.reshape(128, 4, 128)),
        ("ssum", ssum.reshape(128, 32)),
        ("wo", blocks(A["attn_out_proj_w"].T)),
        ("w1", w1),
        ("w2", w2.reshape(3, 128, 128).transpose(1, 0, 2)),
        ("gamma", _np.broadcast_to(A["ffn_gamma"], (128, 128))),
        ("beta", _np.broadcast_to(A["ffn_beta"], (128, 128))),
        ("pathsel", pathsel),
    ]
    nc = _bacc.Bacc("TRN2", target_bir_lowering=False, num_devices=1)
    feeds, args = {}, []
    for name, a in arrays:
        a = _np.ascontiguousarray(a)
        feeds[f"in_{name}"] = a
        args.append(nc.dram_tensor(f"in_{name}", a.shape, _mybir.dt.float32, kind="ExternalInput").ap())
    args.append(nc.dram_tensor("out_y", (8, 1024, 128), _mybir.dt.float32, kind="ExternalOutput").ap())
    build(nc, *args)
    r = _run(nc, [feeds], core_ids=[0])
    return r.results[0]["out_y"]
```
